# Optimizing a Trainium2 kernel written in Bass

```python
import numpy as np
import jax
import jax.numpy as jnp

def _softmax(x, axis=-1):
    return jax.nn.softmax(x, axis=axis)

def _gelu(x):
    return jax.nn.gelu(x, approximate=True)

def _silu(x):
    return jax.nn.silu(x)

def _sigmoid(x):
    return jax.nn.sigmoid(x)

def _layernorm(x, axis=-1, eps=1e-05):
    m = jnp.mean(x, axis=axis, keepdims=True)
    v = jnp.var(x, axis=axis, keepdims=True)
    return (x - m) / jnp.sqrt(v + eps)

def _scatter_add(tgt, idx, src, axis=0):
    return tgt.at[idx].add(src)

def _segment_sum(src, seg, n):
    return jax.ops.segment_sum(src, seg, n)
kernel_name = 'mk_prb_d1_jaxref_r4_fde03d'

def setup_inputs(seed: int=0):
    np.random.seed(seed)
    _w = jnp.asarray

    def _L0_attn_setup():
        import jax, jax.numpy as jnp
        import numpy as np
        B_, L, DM = (2, 512, 256)
        DS = 64
        EXP = 2
        DC = 4
        DI = DM * EXP

        def _forward(x, W_in, conv_w, conv_b, W_x, A_log, D, W_out):
            xz = jnp.einsum('bld,ed->ble', x, W_in)
            x_in, z = jnp.split(xz, 2, axis=-1)
            xc = jnp.transpose(x_in, (0, 2, 1))
            xc = jax.lax.conv_general_dilated(xc, conv_w, window_strides=(1,), padding=[(DC - 1, 0)], dimension_numbers=('NCH', 'OIH', 'NCH'), feature_group_count=DI)
            xc = xc + conv_b[None, :, None]
            xc = jax.nn.silu(jnp.transpose(xc, (0, 2, 1)))
            ssm = jnp.einsum('bld,ed->ble', xc, W_x)
            Bm = ssm[..., :DS]
            Cm = ssm[..., DS:2 * DS]
            dt = jax.nn.softplus(ssm[..., -1])
            A = -jnp.exp(A_log)

            def step(h, inp):
                x_t, B_t, C_t, dt_t = inp
                dtb = dt_t[:, None, None]
                A_bar = jnp.exp(A[None, None, :] * dtb)
                h = A_bar * h + x_t[:, :, None] * (B_t[:, None, :] * dtb)
                y_t = jnp.einsum('bds,bs->bd', h, C_t)
                return (h, y_t)
            h0 = jnp.zeros((x.shape[0], DI, DS), xc.dtype)
            xs = (jnp.swapaxes(xc, 0, 1), jnp.swapaxes(Bm, 0, 1), jnp.swapaxes(Cm, 0, 1), jnp.swapaxes(dt, 0, 1))
            _, ys = jax.lax.scan(step, h0, xs)
            y = jnp.swapaxes(ys, 0, 1)
            y = y + xc * D
            y = y * jax.nn.silu(z)
            return jnp.einsum('bld,od->blo', y, W_out)
        key = jax.random.key(seed)
        ks = jax.random.split(key, 6)
        sc = lambda k, shape, fan: jax.random.normal(k, shape, jnp.float32) * fan ** (-0.5)
        x = jax.random.normal(ks[0], (B_, L, DM), jnp.float32)
        W_in = sc(ks[1], (2 * DI, DM), DM)
        conv_w = sc(ks[2], (DI, 1, DC), DC)
        conv_b = sc(ks[3], (DI,), DC)
        W_x = sc(ks[4], (2 * DS + 1, DI), DI)
        A_log = jnp.log(jnp.arange(1, DS + 1, dtype=jnp.float32))
        D = jnp.ones((DI,), jnp.float32)
        W_out = sc(ks[5], (DM, DI), DI)
        return {'x': x, 'W_in': W_in, 'conv_w': conv_w, 'conv_b': conv_b, 'W_x': W_x, 'A_log': A_log, 'D': D, 'W_out': W_out}
    _L0_attn_in = _L0_attn_setup()

    def _L0_ffn_setup():
        import jax, jax.numpy as jnp
        import numpy as np
        NUM_EXPERTS = 8
        D_MODEL = 256
        D_OUT = 256
        key = jax.random.key(seed)
        ks = jax.random.split(key, 5)
        B, S = (2, 512)
        x = jax.random.normal(ks[0], (B, S, D_MODEL), dtype=jnp.float32)
        gate_w = jax.random.normal(ks[1], (D_MODEL, NUM_EXPERTS), dtype=jnp.float32) * 0.02
        gate_b = jnp.zeros((NUM_EXPERTS,), dtype=jnp.float32)
        expert_w = jax.random.normal(ks[2], (NUM_EXPERTS, D_MODEL, D_OUT), dtype=jnp.float32) * 0.02
        expert_b = jnp.zeros((NUM_EXPERTS, D_OUT), dtype=jnp.float32)
        return {'x': x, 'gate_w': gate_w, 'gate_b': gate_b, 'expert_w': expert_w, 'expert_b': expert_b}
    _L0_ffn_in = _L0_ffn_setup()
    _d = {'L0_attn_x': _L0_attn_in['x'], 'L0_attn_W_in': _L0_attn_in['W_in'], 'L0_attn_conv_w': _L0_attn_in['conv_w'], 'L0_attn_conv_b': _L0_attn_in['conv_b'], 'L0_attn_W_x': _L0_attn_in['W_x'], 'L0_attn_A_log': _L0_attn_in['A_log'], 'L0_attn_D': _L0_attn_in['D'], 'L0_attn_W_out': _L0_attn_in['W_out'], 'L0_ffn_gate_w': _L0_ffn_in['gate_w'], 'L0_ffn_gate_b': _L0_ffn_in['gate_b'], 'L0_ffn_expert_w': _L0_ffn_in['expert_w'], 'L0_ffn_expert_b': _L0_ffn_in['expert_b']}
    _x0 = _d['L0_attn_x']
    _d['L0_attn_x'] = jax.random.normal(jax.random.fold_in(jax.random.key(seed), 1), (32, 512, 256), dtype=_x0.dtype)
    del _x0
    return _d

def reference(L0_attn_x, L0_attn_W_in, L0_attn_conv_w, L0_attn_conv_b, L0_attn_W_x, L0_attn_A_log, L0_attn_D, L0_attn_W_out, L0_ffn_gate_w, L0_ffn_gate_b, L0_ffn_expert_w, L0_ffn_expert_b):

    def _L0_attn_ref(x, W_in, conv_w, conv_b, W_x, A_log, D, W_out):
        import jax, jax.numpy as jnp
        import numpy as np
        B_, L, DM = (2, 512, 256)
        DS = 64
        EXP = 2
        DC = 4
        DI = DM * EXP

        def _forward(x, W_in, conv_w, conv_b, W_x, A_log, D, W_out):
            xz = jnp.einsum('bld,ed->ble', x, W_in)
            x_in, z = jnp.split(xz, 2, axis=-1)
            xc = jnp.transpose(x_in, (0, 2, 1))
            xc = jax.lax.conv_general_dilated(xc, conv_w, window_strides=(1,), padding=[(DC - 1, 0)], dimension_numbers=('NCH', 'OIH', 'NCH'), feature_group_count=DI)
            xc = xc + conv_b[None, :, None]
            xc = jax.nn.silu(jnp.transpose(xc, (0, 2, 1)))
            ssm = jnp.einsum('bld,ed->ble', xc, W_x)
            Bm = ssm[..., :DS]
            Cm = ssm[..., DS:2 * DS]
            dt = jax.nn.softplus(ssm[..., -1])
            A = -jnp.exp(A_log)

            def step(h, inp):
                x_t, B_t, C_t, dt_t = inp
                dtb = dt_t[:, None, None]
                A_bar = jnp.exp(A[None, None, :] * dtb)
                h = A_bar * h + x_t[:, :, None] * (B_t[:, None, :] * dtb)
                y_t = jnp.einsum('bds,bs->bd', h, C_t)
                return (h, y_t)
            h0 = jnp.zeros((x.shape[0], DI, DS), xc.dtype)
            xs = (jnp.swapaxes(xc, 0, 1), jnp.swapaxes(Bm, 0, 1), jnp.swapaxes(Cm, 0, 1), jnp.swapaxes(dt, 0, 1))
            _, ys = jax.lax.scan(step, h0, xs)
            y = jnp.swapaxes(ys, 0, 1)
            y = y + xc * D
            y = y * jax.nn.silu(z)
            return jnp.einsum('bld,od->blo', y, W_out)
        return _forward(x, W_in, conv_w, conv_b, W_x, A_log, D, W_out)

    def _L0_ffn_ref(x, gate_w, gate_b, expert_w, expert_b):
        import jax, jax.numpy as jnp
        import numpy as np
        NUM_EXPERTS = 8
        D_MODEL = 256
        D_OUT = 256
        orig_shape = x.shape
        xt = x.reshape(-1, D_MODEL)
        logits = xt @ gate_w + gate_b
        gates = jax.nn.softmax(logits, axis=-1)
        sel = jnp.argmax(gates, axis=-1)
        onehot = jax.nn.one_hot(sel, NUM_EXPERTS, dtype=xt.dtype)
        y_all = jnp.einsum('td,edh->eth', xt, expert_w) + expert_b[:, None, :]
        out = jnp.einsum('te,eth->th', onehot, y_all)
        return out.reshape(*orig_shape[:-1], D_OUT)
    x = L0_attn_x
    xn = _layernorm(x, axis=-1)
    x = x + _L0_attn_ref(xn, L0_attn_W_in, L0_attn_conv_w, L0_attn_conv_b, L0_attn_W_x, L0_attn_A_log, L0_attn_D, L0_attn_W_out) + _L0_ffn_ref(xn, L0_ffn_gate_w, L0_ffn_gate_b, L0_ffn_expert_w, L0_ffn_expert_b)
    return x

_drawn_inputs = setup_inputs


def setup_inputs(seed=0):
    import zlib

    import numpy as np

    out = dict(_drawn_inputs(seed))
    spreads = {'L0_attn_D': (1.0, 0.2), 'L0_ffn_gate_b': (0.0, 0.1), 'L0_ffn_expert_b': (0.0, 0.1)}
    factors = {}
    for name, (base, spread) in spreads.items():
        noise = np.random.default_rng([zlib.crc32(name.encode()), seed]).standard_normal(out[name].shape)
        drawn = base * np.exp(spread * noise) if base else spread * noise
        out[name] = jnp.asarray(drawn.astype(out[name].dtype))
    for name, factor in factors.items():
        out[name] = (out[name] * factor).astype(out[name].dtype)
    return out
```

```python
from contextlib import ExitStack

import numpy as np

import concourse.bass as bass
from concourse import mybir

P = 128
F32 = mybir.dt.float32
F32R = mybir.dt.float32r
BF16 = mybir.dt.bfloat16
I32 = mybir.dt.int32
U8 = mybir.dt.uint8
ALU = mybir.AluOpType
ACT = mybir.ActivationFunctionType
AX = mybir.AxisListType
EPS = 1e-5

L = 512
DM = 256
DI = 512
DS = 64
DC = 4
E = 8
KB = L // P
QB = 2 * KB
KD = DM // P
CD = DI // P
LEVELS = 7
MAPS = LEVELS + 2
XS_W = DM + 1
NO_TOKEN = 1 << 20

PROJ = 2 * KD + 4 * CD
STAGE_B, STAGE_C = 21, 12
STAGE = STAGE_B + STAGE_C
B_LOGIT, B_BC, B_BT, B_CT, B_LGT, B_EXP, B_RANK = 0, 2, 5, 6, 7, 8, 20
C_TRA, C_XA, C_XB, C_TRB = 21, 25, 27, 29
LEV = 2 * LEVELS
YOUT = 2 * CD + 4
SOFTPLUS = 14
ROUTE = 10
KX = 4
TILE_RING = 8
UNITS = [(0, 0, 0), (0, 0, 1), (0, 1, 1), (0, 1, 0), (0, 2, 0), (0, 2, 1), (0, 3, 1), (0, 3, 0),
         (1, 0, 0), (1, 0, 1), (1, 1, 1), (1, 1, 0), (1, 2, 0), (1, 2, 1), (1, 3, 0), (1, 3, 1)]
LAG = 2
X_UNIT = [UNITS.index((v // CD, v % CD, 0)) for v in range(2 * CD)]


def shape_constants():
    t = np.arange(P)
    smap = np.zeros((P, MAPS, P), np.float32)
    mask = np.zeros((P, LEVELS, P // 2), np.float32)
    src, dst = t[:, None], t[None, :]
    for l in range(LEVELS):
        h = 1 << l
        mid = dst // (2 * h) * (2 * h) + h
        left = dst < mid
        smap[:, l] = np.where(left, (src > dst) & (src < mid), (src >= mid) & (src <= dst))
        right = t[t % (2 * h) >= h][None, :]
        mask[:, l] = (src // (2 * h) == right // (2 * h)) & (src % (2 * h) < h)
    smap[:, LEVELS] = src > dst
    smap[:, LEVELS + 1] = src <= dst
    ident = np.eye(P, dtype=np.float32)
    upper = (src < dst).astype(np.float32)
    code = np.tile(E - np.arange(E, dtype=np.float32), QB)
    reset = np.tile((np.arange(QB) > 0).astype(np.float32), E)
    return smap.reshape(P, -1), mask.reshape(P, -1), ident, upper, code, reset


class Pair:

    def __init__(self, i, off):
        self.i, self.off, self.par = i, off, off % 2

    def plus(self, d):
        return Pair(self.i, self.off + d)

    def count(self, per, k):
        return self.i * (2 * per) + (self.off * per + k)

    def visits(self, per, k=0):
        return self.i * per + (self.off // 2 * per + k)


def after(eng, sem, value):
    if not isinstance(value, int) or value > 0:
        eng.wait_ge(sem, value)


def pass_waits(eng, sem):
    eng.sem_inc(sem, 1)


class Chain:

    def __init__(self, eng, sem, pair, per):
        self.eng, self.sem, self.pair, self.per, self.k = eng, sem, pair, per, 0

    def did(self, ins):
        ins.then_inc(self.sem, 1)
        self.k += 1

    def last(self):
        after(self.eng, self.sem, self.pair.count(self.per, self.k))


def mamba_moe(nc, x, w_in, w_x, w_out, conv, a_row, gate_w, gate_b, ew, eb, smap, mask, ident_d, upper_d,
              rows_d, out):
    T = x.shape[0]
    NPAIR = T // (P * QB)
    CAP = T + P
    DUMMY = E * CAP
    NR = DUMMY + P
    NT = T // P + E
    assert NPAIR % 2 == 0 and NPAIR >= 6 and NT % TILE_RING == 0

    xs_dram = nc.dram_tensor("xs_dram", [NR, XS_W], F32, kind="Internal").ap()
    rs_dram = nc.dram_tensor("rs_dram", [NR, DM], F32, kind="Internal").ap()
    x_pair = x.rearrange("(n q p) d -> n p q d", p=P, q=QB)

    with ExitStack() as ctx:
        def sb(name, shape, dt=F32):
            return ctx.enter_context(nc.sbuf_tensor(name, shape, dt))

        def sem(name):
            return ctx.enter_context(nc.semaphore(name))

        def banks(name):
            return [ctx.enter_context(nc.psum_tensor(f"{name}{i}", [P, 512], F32)) for i in range(2)]

        xn = [sb(f"xn{i}", [P, QB, XS_W]) for i in range(2)]
        stats = sb("stats", [P, QB, 6])
        mv = sb("mv", [P, QB, 2])
        var_eps = sb("var_eps", [P, QB])
        rstd = sb("rstd", [P, QB])
        neg_half = sb("neg_half", [P, QB])
        xt_hi = sb("xt_hi", [P, KD, 2, L], F32R)
        xt_lo = sb("xt_lo", [P, KD, 2, L], F32R)
        xc = [sb(f"xc{i}", [P, CD, 2, L]) for i in range(2)]
        gz = [sb(f"gz{i}", [P, CD, 2, L]) for i in range(2)]
        th_x = [sb(f"th_x{i}", [P, L]) for i in range(2)]
        bc = sb("bc", [P, 2, QB, DS])
        raw_dt = sb("raw_dt", [P, QB])
        sp = [sb(f"sp{i}", [P, QB]) for i in range(8)]
        dta = sb("dta", [P, QB, DS])
        dta_hi = sb("dta_hi", [P, QB, DS], F32R)
        dta_lo = sb("dta_lo", [P, QB, DS], F32R)
        bdt = sb("bdt", [P, QB, DS])
        diag = sb("diag", [P, QB])
        bt = sb("bt", [P, L])
        ct = sb("ct", [P, L])
        fac = sb("fac", [P, MAPS, L])
        tot = sb("tot", [P, 2])
        kx = sb("kx", [P, 2 * P])
        xct = sb("xct", [P, KB, DI])
        gm = sb("gm", [P, 2, KB * L])
        res = sb("res", [P, QB, DM])
        lgt = sb("lgt", [E, 2, L])
        lg = sb("lg", [P, QB, E])
        eq = sb("eq", [P, QB, E])
        oh = sb("oh", [P, E, QB])
        cs = sb("cs", [P, E, QB])
        mx = sb("mx", [P, QB])
        sel = sb("sel", [P, QB])
        rt = sb("rt", [P, E], BF16)
        rk = sb("rk", [P, 2 * E])
        base = sb("base", [P, E])
        b1 = sb("b1", [P, E])
        posf = sb("posf", [P, QB])
        pos = [sb(f"pos{i}", [P, QB], I32) for i in range(2)]
        win_hi = sb("win_hi", [P, KD, 2 * DI], F32R)
        win_lo = sb("win_lo", [P, KD, 2 * DI], F32R)
        wx = sb("wx", [P, CD, 2 * DS + 1])
        wout = sb("wout", [P, CD, DM])
        gate_hi = sb("gate_hi", [P, KD, P], F32R)
        gate_lo = sb("gate_lo", [P, KD, P], F32R)
        smap_r = sb("smap_r", [P, MAPS * P], F32R)
        masks = sb("masks", [P, LEVELS * P // 2], U8)
        ident = sb("ident", [P, P])
        rows = sb("rows", [P, rows_d.shape[1]])
        upper = sb("upper", [P, P], BF16)
        ones = sb("ones", [P, P], BF16)
        convs = sb("convs", [P, CD, DC + 2])
        a_neg = sb("a_neg", [P, DS])
        gb = sb("gb", [E, 1])

        proj_bank, stage_bank, level_bank, yout_bank = (banks(n) for n in ("proj", "stage", "level", "yout"))

        code = rows[:, 0:QB * E].rearrange("p (k e) -> p k e", e=E)
        reset = rows[:, 64:128]
        base0 = rows[:, 128:136]
        tok0 = [rows[:, 136:144], rows[:, 144:152]]
        tile_no = rows[:, 152:152 + NT]
        pad_row = rows[:, 152 + NT:160 + NT]
        w_stage = gm[:, :, :].rearrange("p a n -> p (a n)")
        s_stage = fac[:, :, :].rearrange("p a n -> p (a n)")

        consts_loaded, consts_ready, masks_ready, pool_consts = map(
            sem, ("consts_loaded", "consts_ready", "masks_ready", "pool_consts"))
        x_loaded = [sem(f"x_loaded{i}") for i in range(2)]
        xs_sent = [sem(f"xs_sent{i}") for i in range(2)]
        rs_sent = [sem(f"rs_sent{i}") for i in range(2)]
        res_loaded = sem("res_loaded")
        ln_stats, ln_mv, var_ready, rstd_ready, xn_ready = map(
            sem, ("ln_stats", "ln_mv", "var_ready", "rstd_ready", "xn_ready"))
        proj_full, proj_done, hi_ready = map(sem, ("proj_full", "proj_done", "hi_ready"))
        tap_ready, conv_step, thx_ready, thz_ready, xc_ready = map(
            sem, ("tap_ready", "conv_step", "thx_ready", "thz_ready", "xc_ready"))
        stage_full, stage_copied = map(sem, ("stage_full", "stage_copied"))
        level_full, level_done, gm_cleared = map(sem, ("level_full", "level_done", "gm_cleared"))
        yout_full, yout_done, gated = map(sem, ("yout_full", "yout_done", "gated"))
        softplus_step, exp_ready, dta_ready, split_ready = map(
            sem, ("softplus_step", "exp_ready", "dta_ready", "split_ready"))
        bdt_ready, bdtc_ready, diag_ready, kq_ready, kx_step = map(
            sem, ("bdt_ready", "bdtc_ready", "diag_ready", "kq_ready", "kx_step"))
        route_step, counted, pos_ready = map(sem, ("route_step", "counted", "pos_ready"))

        ew_sb = xc[0][:, :, :, :].rearrange("p a b n -> p (a b n)")
        eb_sb = xc[1][:, :, :, :].rearrange("p a b n -> p (a b n)")[:, 0:E * DM]
        ph2 = [g[:, :, :, :].rearrange("p a b n -> p (a b n)") for g in gz]
        rs_t = [ph2[0][:, r * DM:(r + 1) * DM] for r in range(TILE_RING)]
        xt_t = [ph2[0][:, (TILE_RING + r) * DM:(TILE_RING + r + 1) * DM] for r in range(2)]
        xs_t = [ph2[1][:, r * XS_W:(r + 1) * XS_W] for r in range(TILE_RING)]
        tmp = [ph2[1][:, TILE_RING * XS_W + r * NT:TILE_RING * XS_W + (r + 1) * NT] for r in range(7)]
        prod = yout_bank + level_bank
        tok_i = [pos[0][:, r:r + 1] for r in range(TILE_RING)]
        zero = fac[:, 0, 0:XS_W]
        signal = sb("signal", [1, 8])
        pad_i = sb("pad_i", [P, E], I32)
        tile_i = sb("tile_i", [1, 3 * NT], I32)
        cnt_i = sb("cnt_i", [P, E], I32)
        main_done, table_step, table_ready, pads_ready, pads_sent = map(
            sem, ("main_done", "table_step", "table_ready", "pads_ready", "pads_sent"))
        ew_loaded = sem("ew_loaded")
        tanh_ready = sem("tanh_ready")
        dve_passed, pool_passed = map(sem, ("dve_passed", "pool_passed"))
        a_exp = sem("a_exp")
        xs_got = [sem(f"xs_got{r}") for r in range(TILE_RING)]
        rs_got = [sem(f"rs_got{r}") for r in range(TILE_RING)]
        out_sent = [sem(f"out_sent{r}") for r in range(TILE_RING)]
        t_turned, t_copied, t_product, t_biased, t_tok, t_sum = map(
            sem, ("t_turned", "t_copied", "t_product", "t_biased", "t_tok", "t_sum"))

        block = ctx.enter_context(nc.Block())

        def blk(ap, ab, j):
            return ap[:, :, ab, j * P:(j + 1) * P]

        @block.sync
        def _(sp_eng):
            loads = [(w_stage[:, 0:KD * 2 * DI].rearrange("p (k n) -> p k n", k=KD), w_in.rearrange("(k p) n -> p k n", p=P)),
                     (w_stage[:, 2048:2048 + KD * E].rearrange("p (k n) -> p k n", k=KD),
                      gate_w.rearrange("(k p) n -> p k n", p=P)),
                     (w_stage[:, 2100:2228], upper_d), (s_stage[:, 0:MAPS * P], smap),
                     (s_stage[:, 2048:2048 + LEVELS * P // 2], mask),
                     (wx[:, :, :], w_x.rearrange("(c p) n -> p c n", p=P)),
                     (wout[:, :, :], w_out.rearrange("(c p) n -> p c n", p=P)),
                     (convs[:, :, :], conv.rearrange("(c p) n -> p c n", p=P)),
                     (ident[:, :], ident_d), (rows[:, :], rows_d), (a_neg[:, :], a_row), (gb[:, :], gate_b)]
            for dst, src in loads:
                sp_eng.dma_start(dst, src).then_inc(consts_loaded, 16)
            for par in range(2):
                sp_eng.dma_start(xn[par][:, :, 0:DM], x_pair[par]).then_inc(x_loaded[par], 16)
            sp_eng.dma_start(res[:, :, :], x_pair[0]).then_inc(res_loaded, 16)

            def pair_loads(n):
                nxt = n.plus(2)
                after(sp_eng, xs_sent[n.par], n.visits(16 * QB, 16 * QB))
                sp_eng.dma_start(xn[n.par][:, :, 0:DM], x_pair[nxt.i * 2 + nxt.off]).then_inc(x_loaded[n.par], 16)
                after(sp_eng, rs_sent[n.par], n.visits(16 * QB, 16 * QB))
                sp_eng.dma_start(res[:, :, :], x_pair[n.i * 2 + n.off + 1]).then_inc(res_loaded, 16)

            with sp_eng.Fori(0, NPAIR // 2 - 1) as i:
                pair_loads(Pair(i, 0))
                pair_loads(Pair(i, 1))
            after(sp_eng, rs_sent[0], 16 * QB * (NPAIR // 2))
            sp_eng.dma_start(res[:, :, :], x_pair[NPAIR - 1]).then_inc(res_loaded, 16)

            sp_eng.wait_ge(main_done, 1)
            sp_eng.dma_start(ew_sb.rearrange("p (e k n) -> p e k n", e=E, k=KD),
                             ew.rearrange("e (k p) n -> p e k n", p=P)).then_inc(ew_loaded, 16)
            sp_eng.dma_start(eb_sb, eb).then_inc(ew_loaded, 16)
            for par in range(2):
                sp_eng.wait_ge(xs_sent[par], 16 * QB * (NPAIR // 2))
                sp_eng.wait_ge(rs_sent[par], 16 * QB * (NPAIR // 2))
            sp_eng.wait_ge(pads_sent, 32 * (E + 1))
            sp_eng.wait_ge(table_ready, 1)

            def load_tile(t, r):
                row = sp_eng.value_load(tile_i[0:1, bass.ds(t, 1)], min_val=0, max_val=NR - P)
                sp_eng.dma_start(xs_t[r], xs_dram[bass.ds(row, P), :]).then_inc(xs_got[r], 16)
                sp_eng.dma_start(rs_t[r], rs_dram[bass.ds(row, P), :]).then_inc(rs_got[r], 16)

            for r in range(TILE_RING):
                load_tile(r, r)
            with sp_eng.Fori(0, NT // TILE_RING - 1) as i:
                for r in range(TILE_RING):
                    sp_eng.wait_ge(out_sent[r], i * 16 + 16)
                    load_tile(i * TILE_RING + (TILE_RING + r), r)

        @block.tensor
        def _(pe):
            class Use:
                def __init__(self, banks, full, done):
                    self.banks, self.full, self.done = banks, full, done

                def begin(self, pair, per, k):
                    after(pe, self.done, pair.count(per, k - 1))
                    return self.banks[(pair.off * per + k) % 2]

            proj = Use(proj_bank, proj_full, proj_done)
            stage = Use(stage_bank, stage_full, stage_copied)
            level = Use(level_bank, level_full, level_done)
            yout = Use(yout_bank, yout_full, yout_done)

            def turn_x(m, ab, k):
                u = ab * KD + k
                if u == 0:
                    after(pe, xn_ready, m.count(1, 1))
                ps = proj.begin(m, PROJ, u)
                for j in range(KB):
                    ins = pe.transpose(ps[:, j * P:(j + 1) * P], xn[m.par][:, ab * KB + j, k * P:(k + 1) * P], ident[:, :])
                ins.then_inc(proj_full, 1)

            def project(m, u):
                ab, c, isz = UNITS[u]
                if u % 8 == 0:
                    after(pe, proj_done, m.count(PROJ, (ab + 1) * KD))
                ps = proj.begin(m, PROJ, 2 * KD + u)
                w = slice((isz * CD + c) * P, (isz * CD + c + 1) * P)
                n = 0
                for k in range(KD):
                    for wi, xi in ((win_hi, xt_hi), (win_hi, xt_lo), (win_lo, xt_hi)):
                        ins = pe.matmul(ps[:, :], wi[:, k, w], xi[:, k, ab, :], start=(n == 0), stop=(n == 3 * KD - 1))
                        n += 1
                ins.then_inc(proj_full, 1)

            def token_products(m, g):
                if g == 0:
                    after(pe, xc_ready, m.count(2 * CD, 2 * CD))
                ps = stage.begin(m, STAGE, B_BC + g)
                w = 2 * DS + 1
                for s, q in enumerate(range(3 * g, min(3 * g + 3, QB))):
                    j, ab = q // 2, q % 2
                    for c in range(CD):
                        ins = pe.matmul(ps[:, s * w:(s + 1) * w], blk(xc[m.par], ab, j)[:, c, :], wx[:, c, :],
                                        start=(c == 0), stop=(c == CD - 1))
                ins.then_inc(stage_full, 1)

            def logits(m, ab):
                ps = stage.begin(m, STAGE, B_LOGIT + ab)
                n = 0
                for k in range(KD):
                    for wi, xi in ((gate_hi, xt_hi), (gate_hi, xt_lo), (gate_lo, xt_hi)):
                        ins = pe.matmul(ps[:, :], wi[:, k, :], xi[:, k, ab, :], start=(n == 0), stop=(n == 3 * KD - 1))
                        n += 1
                ins.then_inc(stage_full, 1)

            def turn_states(m, u, src):
                ps = stage.begin(m, STAGE, u)
                for j in range(KB):
                    ins = pe.transpose(ps[:, j * P:(j + 1) * P], src[:, 2 * j:2 * j + 2, :], ident[:, :])
                ins.then_inc(stage_full, 1)

            def turn_logits(m):
                after(pe, stage_copied, m.count(STAGE, B_LOGIT + 2))
                ps = stage.begin(m, STAGE, B_LGT)
                for q in range(QB):
                    ins = pe.matmul(ps[:, q * E:(q + 1) * E], lgt[:, q // KB, q % KB * P:(q % KB + 1) * P],
                                    ident[0:E, 0:E], start=True, stop=True)
                ins.then_inc(stage_full, 1)

            def exponents(m, e):
                third, j = e // KB, e % KB
                if e == 0:
                    after(pe, split_ready, m.count(2, 2))
                ps = stage.begin(m, STAGE, B_EXP + e)
                w = MAPS // 3 * P
                for n, d in enumerate((dta_hi, dta_lo)):
                    ins = pe.matmul(ps[:, 0:w], d[:, 2 * j:2 * j + 2, :], smap_r[:, third * w:(third + 1) * w],
                                    start=(n == 0), stop=(n == 1))
                ins.then_inc(stage_full, 1)

            def rank(m):
                after(pe, counted, m.count(1, 1))
                ps = stage.begin(m, STAGE, B_RANK)
                pe.matmul(ps[:, 0:E], upper[:, :], rt[:, :], start=True, stop=True)
                pe.matmul(ps[:, E:2 * E], ones[:, :], rt[:, :], start=True, stop=True).then_inc(stage_full, 1)

            def turn_xc(n, ab, j):
                ps = stage.begin(n, STAGE, (C_TRB if ab else C_TRA) + j)
                for c in range(CD):
                    ins = pe.transpose(ps[:, c * P:(c + 1) * P], blk(xc[n.par], ab, j)[:, c, :], ident[:, :])
                ins.then_inc(stage_full, 1)

            def score(n, ab, l):
                after(pe, kq_ready, n.count(LEVELS, l + 1))
                ps = level.begin(n, LEV, ab * LEVELS + l)
                for j in range(KB):
                    kq = fac[ab * DS:(ab + 1) * DS, l, j * P:(j + 1) * P]
                    right = kq.rearrange("p (g t h) -> p g t h", t=2, h=1 << l)[:, :, 1, :]
                    ins = pe.matmul(ps[:, j * P // 2:(j + 1) * P // 2], kq, right, start=True, stop=True)
                ins.then_inc(level_full, 1)

            def cross(n, ab):
                if ab == 0:
                    after(pe, kx_step, n.count(KX, KX))
                s = slice(ab * DS, (ab + 1) * DS)
                pre, suf = fac[s, LEVELS + 1, :], fac[s, LEVELS, :]
                ps = stage.begin(n, STAGE, (C_XB if ab else C_XA))
                pe.matmul(ps[:, 0:P], suf[:, 0:P], pre[:, P:2 * P], start=True, stop=True)
                pe.matmul(ps[:, P:3 * P], pre[:, 0:P], kx[s, :], start=True, stop=True).then_inc(stage_full, 1)
                ps = stage.begin(n, STAGE, (C_XB if ab else C_XA) + 1)
                pe.matmul(ps[:, 0:2 * P], suf[:, P:2 * P], kx[s, :], start=True, stop=True)
                pe.matmul(ps[:, 2 * P:3 * P], suf[:, 2 * P:3 * P], pre[:, 3 * P:4 * P], start=True,
                          stop=True).then_inc(stage_full, 1)

            def product_y(n, ab, c):
                if c == 0:
                    after(pe, level_done, n.count(LEV, (ab + 1) * LEVELS))
                    after(pe, stage_copied, n.count(STAGE, (C_TRB if ab else C_XB)  + (KB if ab else 0)))
                ps = yout.begin(n, YOUT, ab * CD + c)
                for j in range(KB):
                    ins = pe.matmul(ps[:, j * P:L], xct[:, j, c * P:(c + 1) * P],
                                    gm[:, ab, j * L:(j + 1) * L - j * P], start=(j == 0), stop=(j == KB - 1))
                ins.then_inc(yout_full, 1)

            def product_out(n, o):
                ab, half = o // 2, o % 2
                if half == 0:
                    after(pe, gated, n.count(2 * CD, (ab + 1) * CD))
                ps = yout.begin(n, YOUT, 2 * CD + o)
                for s in range(2):
                    for c in range(CD):
                        ins = pe.matmul(ps[:, s * DM:(s + 1) * DM], blk(gz[n.par], ab, 2 * half + s)[:, c, :],
                                        wout[:, c, :], start=(c == 0), stop=(c == CD - 1))
                ins.then_inc(yout_full, 1)

            def step(n, do_ab, do_cd):
                m = n.plus(1)
                if do_ab:
                    turn_x(m, 0, 0), turn_x(m, 0, 1)
                if do_cd:
                    for j in range(KB):
                        turn_xc(n, 0, j)
                if do_ab:
                    turn_x(m, 1, 0), turn_x(m, 1, 1)
                for u in range(8):
                    if do_cd and u < LEVELS:
                        score(n, 0, u)
                    if do_ab:
                        project(m, u)
                if do_cd:
                    cross(n, 0), cross(n, 1)
                for u in range(8):
                    if do_ab:
                        project(m, 8 + u)
                    if do_cd and u < LEVELS:
                        score(n, 1, u)
                    if do_cd and u % 2:
                        product_y(n, 0, u // 2)
                if do_cd:
                    for j in range(KB):
                        turn_xc(n, 1, j)
                    product_y(n, 1, 0)
                if do_ab:
                    logits(m, 0), logits(m, 1)
                if do_cd:
                    product_y(n, 1, 1)
                if do_ab:
                    for g in range(3):
                        token_products(m, g)
                if do_cd:
                    product_y(n, 1, 2)
                if do_ab:
                    after(pe, bdt_ready, m.count(1, 1))
                    turn_states(m, B_BT, bdt)
                    turn_states(m, B_CT, bc[:, 1, :, :])
                    turn_logits(m)
                if do_cd:
                    product_y(n, 1, 3)
                for e in range(12):
                    if do_ab:
                        exponents(m, e)
                    if do_cd and e in (5, 9):
                        product_out(n, e // 8)
                if do_ab:
                    rank(m)
                if do_cd:
                    product_out(n, 2), product_out(n, 3)

            pe.wait_ge(consts_ready, 1)
            pe.wait_ge(pool_consts, 2)
            step(Pair(0, -1), True, False)
            step(Pair(0, 0), True, True)
            with pe.Fori(0, NPAIR // 2 - 2) as i:
                step(Pair(i, 1), True, True)
                step(Pair(i, 2), True, True)
            step(Pair(0, NPAIR - 3), True, True)
            step(Pair(0, NPAIR - 2), True, True)
            step(Pair(0, NPAIR - 1), False, True)

            pe.wait_ge(ew_loaded, 32)
            pe.wait_ge(table_ready, 1)

            def turn_tile(r):
                ps = proj_bank[r % 2]
                pe.transpose(ps[:, 0:P], xs_t[r][:, 0:P], ident[:, :])
                pe.transpose(ps[:, P:2 * P], xs_t[r][:, P:2 * P], ident[:, :]).then_inc(t_turned, 1)

            with pe.Fori(0, NT // TILE_RING) as i:
                pe.wait_ge(xs_got[0], i * 16 + 16)
                turn_tile(0)
                for r in range(TILE_RING):
                    col = pe.value_load(tile_i[0:1, bass.ds(i * TILE_RING + (NT + r), 1)], min_val=0, max_val=(E - 1) * KD * DM)
                    if r < TILE_RING - 1:
                        pe.wait_ge(xs_got[r + 1], i * 16 + 16)
                        turn_tile(r + 1)
                    pe.wait_ge(t_copied, i * TILE_RING + (r + 1))
                    pe.wait_ge(t_sum, i * TILE_RING + (r + 1))
                    py = prod[r % 4]
                    for k in range(KD):
                        ins = pe.matmul(py[:, 0:DM], xt_t[r % 2][:, k * P:(k + 1) * P],
                                        ew_sb[:, bass.ds(col + k * DM, DM)], start=(k == 0), stop=(k == KD - 1))
                    ins.then_inc(t_product, 1)

        @block.scalar
        def _(act):
            def staged(pair, k, out_ap, in_ap, fn=ACT.Copy, **kw):
                after(act, stage_full, pair.count(STAGE, k + 1))
                act.activation(out_ap, in_ap, fn, **kw).then_inc(stage_copied, 1)

            def bank(pair, k):
                return stage_bank[(pair.off * STAGE + k) % 2]

            def high_part(m, u):
                after(act, proj_full, m.count(PROJ, u + 1))
                act.activation(xt_hi[:, u % KD, u // KD, :], proj_bank[u % 2][:, :], ACT.Copy).then_inc(hi_ready, 1)

            def unit(m, u):
                ab, c, isz = UNITS[u]
                if u == 0:
                    after(act, gated, m.plus(-2).count(2 * CD, 2 * CD))
                if u == 1:
                    after(act, yout_full, m.plus(-2).count(YOUT, YOUT))
                after(act, proj_full, m.count(PROJ, 2 * KD + u + 1))
                if isz:
                    act.activation(gz[m.par][:, c, ab, :], proj_bank[u % 2][:, :], ACT.Tanh,
                                   scale=0.5).then_inc(thz_ready, 1)
                else:
                    act.activation(xc[m.par][:, c, ab, :], proj_bank[u % 2][:, :], ACT.Identity,
                                   scale=convs[:, c, DC - 1:DC], bias=convs[:, c, DC:DC + 1]).then_inc(tap_ready, 1)

            def tanh_x(m, v):
                after(act, proj_done, m.count(PROJ, 2 * KD + X_UNIT[v] + 1))
                after(act, xc_ready, m.count(2 * CD, v - 1))
                t = th_x[v % 2][:, :]
                act.activation(t, xc[m.par][:, v % CD, v // CD, :], ACT.Tanh, scale=0.5).then_inc(tanh_ready, 1)
                after(act, tanh_ready, m.count(2 * CD, v + 1))
                act.activation(t, t, ACT.Copy, bias=1.0).then_inc(thx_ready, 1)

            def units(m, us):
                for u in us:
                    unit(m, u)
                    for v in range(2 * CD):
                        if X_UNIT[v] == u - LAG:
                            tanh_x(m, v)

            def cross_copy(n, ab):
                k = C_XB if ab else C_XA
                after(act, yout_full, n.plus(-1).count(YOUT, (ab + 1) * CD))
                staged(n, k, gm[:, ab, P:L], bank(n, k)[:, 0:3 * P])
                after(act, stage_full, n.count(STAGE, k + 2))
                act.activation(gm[:, ab, L + P:L + 3 * P], bank(n, k + 1)[:, 0:2 * P], ACT.Copy)
                act.activation(gm[:, ab, 2 * L + P:2 * L + 2 * P], bank(n, k + 1)[:, 2 * P:3 * P],
                               ACT.Copy).then_inc(stage_copied, 1)

            def step(n, do_ab, do_cd):
                m = n.plus(1)
                if do_ab:
                    high_part(m, 0), high_part(m, 1)
                if do_cd:
                    for j in range(KB):
                        staged(n, C_TRA + j, xct[:, j, :], bank(n, C_TRA + j)[:, :])
                if do_ab:
                    high_part(m, 2), high_part(m, 3)
                    units(m, range(8))
                if do_cd:
                    cross_copy(n, 0), cross_copy(n, 1)
                if do_ab:
                    units(m, range(8, 16))
                    for v in range(2 * CD):
                        if X_UNIT[v] > 15 - LAG:
                            tanh_x(m, v)
                if do_cd:
                    for j in range(KB):
                        staged(n, C_TRB + j, xct[:, j, :], bank(n, C_TRB + j)[:, :])
                if do_ab:
                    w = 2 * DS + 1
                    after(act, bdtc_ready, m.plus(-1).count(1, 1))
                    for ab in range(2):
                        staged(m, B_LOGIT + ab, lgt[:, ab, :], bank(m, B_LOGIT + ab)[0:E, :], ACT.Identity, bias=gb[:, :])
                    for g in range(3):
                        nq = min(3, QB - 3 * g)
                        after(act, stage_full, m.count(STAGE, B_BC + g + 1))
                        ps = bank(m, B_BC + g)[:, 0:nq * w].rearrange("p (q n) -> p q n", n=w)
                        for t in range(2):
                            act.activation(bc[:, t, 3 * g:3 * g + nq, :], ps[:, :, t * DS:(t + 1) * DS], ACT.Copy)
                        act.activation(raw_dt[:, 3 * g:3 * g + nq], ps[:, :, 2 * DS], ACT.Copy).then_inc(stage_copied, 1)
                    after(act, softplus_step, m.count(SOFTPLUS, 1))
                    act.activation(sp[1][:, :], sp[0][:, :], ACT.Exp).then_inc(exp_ready, 1)
                    after(act, kx_step, m.plus(-1).count(KX, KX))
                    staged(m, B_BT, bt[:, :], bank(m, B_BT)[:, :])
                    staged(m, B_CT, ct[:, :], bank(m, B_CT)[:, :])
                    staged(m, B_LGT, lg[:, :, :], bank(m, B_LGT)[:, 0:QB * E].rearrange("p (q e) -> p q e", e=E))
                    t = MAPS // 3
                    for e in range(12):
                        third, j = e // KB, e % KB
                        staged(m, B_EXP + e, fac[:, third * t:(third + 1) * t, j * P:(j + 1) * P],
                               bank(m, B_EXP + e)[:, 0:t * P].rearrange("p (t n) -> p t n", n=P), ACT.Exp)
                    staged(m, B_RANK, rk[:, :], bank(m, B_RANK)[:, 0:2 * E])

            act.wait_ge(consts_loaded, 16 * 12)
            act.activation(a_neg[:, :], a_neg[:, :], ACT.Exp).then_inc(a_exp, 1)
            act.wait_ge(consts_ready, 1)
            step(Pair(0, -1), True, False)
            step(Pair(0, 0), True, True)
            with act.Fori(0, NPAIR // 2 - 2) as i:
                step(Pair(i, 1), True, True)
                step(Pair(i, 2), True, True)
            step(Pair(0, NPAIR - 3), True, True)
            step(Pair(0, NPAIR - 2), True, True)
            step(Pair(0, NPAIR - 1), False, True)

            with act.Fori(0, NT // TILE_RING) as i:
                for r in range(TILE_RING):
                    act.wait_ge(t_turned, i * TILE_RING + (r + 1))
                    act.activation(xt_t[r % 2], proj_bank[r % 2][:, 0:DM], ACT.Copy).then_inc(t_copied, 1)

        @block.vector
        def _(dve):
            def ln_stats_of(l):
                after(dve, x_loaded[l.par], l.visits(16, 16))
                for q in range(QB):
                    ins = dve.bn_stats(stats[:, q, :], xn[l.par][:, q, 0:DM])
                ins.then_inc(ln_stats, 1)
                after(dve, ln_stats, l.count(1, 1))
                pass_waits(dve, dve_passed)
                for q in range(QB):
                    ins = dve.bn_aggr(mv[:, q, :], stats[:, q, :])
                ins.then_inc(ln_mv, 1)

            def ln_apply(l, first=False):
                after(dve, rstd_ready, l.count(1, 1))
                if first:
                    dve.tensor_copy(xn[l.par][:, :, DM], tok0[l.par])
                else:
                    dve.tensor_scalar(xn[l.par][:, :, DM], xn[l.par][:, :, DM], float(2 * QB * P), None, ALU.add)
                for q in range(QB):
                    v = xn[l.par][:, q, 0:DM]
                    ins = dve.tensor_scalar(v, v, mv[:, q, 0:1], rstd[:, q:q + 1], ALU.subtract, ALU.mult)
                ins.then_inc(xn_ready, 1)

            def low_part(m, u):
                after(dve, hi_ready, m.count(2 * KD, u + 1))
                dve.tensor_tensor(xt_lo[:, u % KD, u // KD, :], proj_bank[u % 2][:, :],
                                  xt_hi[:, u % KD, u // KD, :].bitcast(F32), ALU.subtract).then_inc(proj_done, 1)

            def conv(m, u):
                ab, c, _ = UNITS[u]
                out_c, k = xc[m.par][:, c, ab, :], 2 * (ab * CD + c)
                after(dve, tap_ready, m.count(2 * CD, ab * CD + c + 1))
                for s in range(1, DC):
                    if s > 1:
                        after(dve, conv_step, m.count(4 * CD, k + s - 1))
                    ins = dve.scalar_tensor_tensor(out_c[:, s:L], proj_bank[u % 2][:, 0:L - s],
                                                   convs[:, c, DC - 1 - s:DC - s], out_c[:, s:L], ALU.mult, ALU.add)
                    ins.then_inc(conv_step if s < DC - 1 else proj_done, 1)

            def project(m, u):
                ab, c, isz = UNITS[u]
                if not isz:
                    conv(m, u)
                else:
                    after(dve, thz_ready, m.count(2 * CD, ab * CD + c + 1))
                    part = gz[m.par][:, c, ab, :]
                    dve.scalar_tensor_tensor(part, part, 1.0, proj_bank[u % 2][:, :], ALU.add, ALU.mult).then_inc(proj_done, 1)

            def clear_gm(n, ab):
                if ab == 0:
                    after(dve, diag_ready, n.count(1, 1))
                after(dve, yout_full, n.plus(-1).count(YOUT, (ab + 1) * CD))
                for j in range(KB):
                    ins = dve.tensor_scalar(gm[:, ab, j * L:j * L + P], ident[:, :], diag[:, 2 * j + ab:2 * j + ab + 1],
                                            None, ALU.mult)
                ins.then_inc(gm_cleared, 1)

            def mask_level(n, ab, l):
                u = ab * LEVELS + l
                after(dve, level_full, n.count(LEV, u + 1))
                if l:
                    after(dve, level_done, n.count(LEV, u))
                else:
                    after(dve, gm_cleared, n.count(2, ab + 1))
                dve.wait_ge(masks_ready, 1)
                pass_waits(dve, dve_passed)
                h, g, w = 1 << l, P // 2 >> l, P // 2
                right = gm[:, ab, :].rearrange("p (j g t h) -> p j g t h", j=KB, t=2, h=h)[:, :, 0:g, 1, :]
                dve.copy_predicated(right, masks[:, l * w:(l + 1) * w].rearrange("p (g h) -> p g h", h=h).unsqueeze(1)
                                    .to_broadcast([P, KB, g, h]),
                                    level_bank[u % 2][:, 0:KB * w].rearrange("p (j g h) -> p j g h", j=KB, h=h)
                                    ).then_inc(level_done, 1)

            def gate_y(n, ab, c):
                u = ab * CD + c
                y, g = xc[n.par][:, c, ab, :], gz[n.par][:, c, ab, :]
                after(dve, yout_full, n.count(YOUT, u + 1))
                dve.scalar_tensor_tensor(y, y, convs[:, c, DC + 1:DC + 2], yout_bank[u % 2][:, :], ALU.mult,
                                         ALU.add).then_inc(yout_done, 1)
                after(dve, yout_done, n.count(YOUT, u + 1))
                dve.tensor_tensor(g, g, y, ALU.mult).then_inc(gated, 1)

            def add_residual(n, o):
                after(dve, yout_full, n.count(YOUT, 2 * CD + o + 1))
                if o == 0:
                    after(dve, res_loaded, n.count(16, 16))
                r = res[:, 2 * o:2 * o + 2, :]
                dve.tensor_tensor(r, yout_bank[o % 2][:, :].rearrange("p (q d) -> p q d", q=2), r,
                                  ALU.add).then_inc(yout_done, 1)

            raw = raw_dt[:, :]

            def softplus_start(m):
                after(dve, stage_copied, m.count(STAGE, B_BC + 3))
                ch = Chain(dve, softplus_step, m, SOFTPLUS)
                ch.did(dve.scalar_tensor_tensor(sp[0][:, :], raw, -1.0, raw, ALU.mult, ALU.min))
                ch.did(dve.tensor_scalar(sp[2][:, :], raw, 0.0, None, ALU.max))
                return ch

            def softplus_end(m, ch):
                after(dve, exp_ready, m.count(1, 1))
                ch.did(dve.tensor_scalar(sp[3][:, :], sp[1][:, :], 2.0, None, ALU.add))
                ch.last()
                ch.did(dve.reciprocal(sp[4][:, :], sp[3][:, :]))
                ch.last()
                ch.did(dve.tensor_tensor(sp[5][:, :], sp[1][:, :], sp[4][:, :], ALU.mult))
                ch.last()
                ch.did(dve.tensor_tensor(sp[6][:, :], sp[5][:, :], sp[5][:, :], ALU.mult))
                ch.last()
                ch.did(dve.tensor_scalar(sp[7][:, :], sp[6][:, :], 1.0 / 13, None, ALU.mult))
                for k in (11, 9, 7, 5, 3):
                    ch.last()
                    ch.did(dve.scalar_tensor_tensor(sp[7][:, :], sp[7][:, :], 1.0 / k, sp[6][:, :], ALU.add, ALU.mult))
                ch.last()
                ch.did(dve.scalar_tensor_tensor(sp[3][:, :], sp[7][:, :], 1.0, sp[5][:, :], ALU.add, ALU.mult))
                ch.last()
                ch.did(dve.scalar_tensor_tensor(sp[4][:, :], sp[3][:, :], 2.0, sp[2][:, :], ALU.mult, ALU.add))
                assert ch.k == SOFTPLUS
                ch.last()
                dve.tensor_tensor(dta[:, :, :], a_neg[:, :].unsqueeze(1).to_broadcast([P, QB, DS]),
                                  sp[4][:, :].unsqueeze(2).to_broadcast([P, QB, DS]), ALU.mult).then_inc(dta_ready, 1)
                after(dve, dta_ready, m.count(1, 1))
                dve.tensor_copy(dta_hi[:, :, :], dta[:, :, :]).then_inc(split_ready, 1)
                after(dve, split_ready, m.count(2, 1))
                dve.tensor_tensor(dta_lo[:, :, :], dta[:, :, :], dta_hi[:, :, :].bitcast(F32),
                                  ALU.subtract).then_inc(split_ready, 1)

            def route_count(m):
                ch = Chain(dve, route_step, m, ROUTE)
                after(dve, stage_copied, m.count(STAGE, B_LGT + 1))
                wide = [P, QB, E]
                ch.did(dve.tensor_reduce(mx[:, :], lg[:, :, :], AX.X, ALU.max))
                ch.last()
                ch.did(dve.tensor_tensor(eq[:, :, :], lg[:, :, :], mx[:, :].unsqueeze(2).to_broadcast(wide), ALU.is_equal))
                ch.last()
                ch.did(dve.tensor_tensor(eq[:, :, :], eq[:, :, :], code, ALU.mult))
                ch.last()
                ch.did(dve.tensor_reduce(sel[:, :], eq[:, :, :], AX.X, ALU.max))
                ch.last()
                ch.did(dve.tensor_tensor(oh[:, :, :].rearrange("p e q -> p q e"), code,
                                         sel[:, :].unsqueeze(2).to_broadcast(wide), ALU.is_equal))
                ch.last()
                ch.did(dve.tensor_tensor_scan(cs[:, :, :].rearrange("p e q -> p (e q)"), reset,
                                              oh[:, :, :].rearrange("p e q -> p (e q)"), 0.0, ALU.mult, ALU.add))
                ch.last()
                dve.tensor_copy(rt[:, :], cs[:, :, QB - 1]).then_inc(counted, 1)
                return ch

            def route_place(m, ch):
                after(dve, stage_copied, m.count(STAGE, B_RANK + 1))
                after(dve, pos_ready, m.count(1, 0))
                ch.did(dve.tensor_tensor(b1[:, :], base[:, :], rk[:, 0:E], ALU.add))
                ch.last()
                ch.did(dve.tensor_tensor(cs[:, :, :], cs[:, :, :], b1[:, :].unsqueeze(2).to_broadcast([P, E, QB]), ALU.add))
                ch.last()
                ch.did(dve.tensor_tensor(cs[:, :, :], cs[:, :, :], oh[:, :, :], ALU.mult))
                ch.last()
                ch.did(dve.tensor_reduce(posf[:, :], cs[:, :, :].rearrange("p e q -> p q e"), AX.X, ALU.add))
                assert ch.k == ROUTE
                dve.tensor_tensor(base[:, :], base[:, :], rk[:, E:2 * E], ALU.add)
                ch.last()
                after(dve, xs_sent[m.par], m.visits(16 * QB))
                after(dve, rs_sent[m.par], m.visits(16 * QB))
                dve.tensor_copy(pos[m.par][:, :], posf[:, :]).then_inc(pos_ready, 1)

            def scale_level(m, l):
                h = 1 << l
                after(dve, stage_copied, m.count(STAGE, B_EXP + (l // (MAPS // 3) + 1) * KB))
                f, b, c = (v.rearrange("p (g t h) -> p g t h", t=2, h=h) for v in (fac[:, l, :], bt[:, :], ct[:, :]))
                dve.tensor_tensor(f[:, :, 0, :], f[:, :, 0, :], b[:, :, 0, :], ALU.mult)
                dve.tensor_tensor(f[:, :, 1, :], f[:, :, 1, :], c[:, :, 1, :], ALU.mult).then_inc(kq_ready, 1)

            def scale_between(m):
                suf, pre = fac[:, LEVELS, :], fac[:, LEVELS + 1, :]
                dve.tensor_copy(tot[:, :], pre.rearrange("p (j n) -> p j n", n=P)[:, 1:3, P - 1]).then_inc(kx_step, 1)
                dve.tensor_tensor(suf, suf, bt[:, :], ALU.mult).then_inc(kx_step, 1)
                after(dve, kx_step, m.count(KX, 1))
                dve.tensor_tensor(pre, pre, ct[:, :], ALU.mult).then_inc(kx_step, 1)
                after(dve, kx_step, m.count(KX, 3))
                dve.tensor_copy(kx[:, 0:P], pre[:, 2 * P:3 * P])
                dve.tensor_scalar(kx[:, P:2 * P], pre[:, 3 * P:4 * P], tot[:, 1:2], None, ALU.mult)
                dve.tensor_scalar(pre[:, 0:P], suf[:, 0:P], tot[:, 0:1], None, ALU.mult).then_inc(kx_step, 1)

            def sum_diag(m):
                after(dve, bdtc_ready, m.count(1, 1))
                dve.tensor_reduce(diag[:, :], dta[:, :, :], AX.X, ALU.add).then_inc(diag_ready, 1)

            def step(n, do_ab, do_cd, do_ln):
                m, l = n.plus(1), n.plus(2)
                if do_ab:
                    low_part(m, 0), low_part(m, 1)
                if do_cd:
                    clear_gm(n, 0)
                if do_ab:
                    low_part(m, 2), low_part(m, 3)
                for u in range(8):
                    if do_cd and u < LEVELS:
                        mask_level(n, 0, u)
                    if do_ab:
                        project(m, u)
                if do_cd:
                    clear_gm(n, 1)
                for u in range(8):
                    if do_ab:
                        project(m, 8 + u)
                    if do_cd and u < LEVELS:
                        mask_level(n, 1, u)
                    if do_cd and u % 2:
                        gate_y(n, 0, u // 2)
                if do_ln:
                    ln_stats_of(l)
                if do_cd:
                    gate_y(n, 1, 0)
                if do_ab:
                    ch = softplus_start(m)
                if do_cd:
                    gate_y(n, 1, 1)
                if do_ab:
                    softplus_end(m, ch)
                if do_cd:
                    gate_y(n, 1, 2)
                if do_ab:
                    ch = route_count(m)
                if do_cd:
                    gate_y(n, 1, 3)
                if do_ab:
                    sum_diag(m)
                    for lv in range(3):
                        scale_level(m, lv)
                if do_cd:
                    add_residual(n, 0)
                if do_ab:
                    for lv in range(3, 6):
                        scale_level(m, lv)
                if do_ln:
                    ln_apply(l, first=do_ln == "first")
                if do_cd:
                    add_residual(n, 1)
                if do_ab:
                    scale_level(m, 6)
                    scale_between(m)
                    route_place(m, ch)
                if do_cd:
                    add_residual(n, 2), add_residual(n, 3)

            dve.wait_ge(consts_loaded, 16 * 12)
            for hi, lo, src in ((win_hi, win_lo, w_stage[:, 0:KD * 2 * DI].rearrange("p (k n) -> p k n", k=KD)),):
                dve.tensor_copy(hi[:, :, :], src).then_inc(table_step, 1)
                dve.wait_ge(table_step, 1)
                dve.tensor_tensor(lo[:, :, :], src, hi[:, :, :].bitcast(F32), ALU.subtract)
            gsrc = w_stage[:, 2048:2048 + KD * E].rearrange("p (k n) -> p k n", k=KD)
            dve.memset(gate_hi[:, :, :].bitcast(F32), 0.0)
            dve.memset(gate_lo[:, :, :].bitcast(F32), 0.0).then_inc(table_step, 1)
            dve.wait_ge(table_step, 2)
            dve.tensor_copy(gate_hi[:, :, 0:E], gsrc).then_inc(table_step, 1)
            dve.wait_ge(table_step, 3)
            dve.tensor_tensor(gate_lo[:, :, 0:E], gsrc, gate_hi[:, :, 0:E].bitcast(F32), ALU.subtract)
            dve.tensor_copy(smap_r[:, :], s_stage[:, 0:MAPS * P])
            dve.tensor_copy(upper[:, :], w_stage[:, 2100:2228])
            dve.tensor_copy(masks[:, :], s_stage[:, 2048:2048 + LEVELS * P // 2]).then_inc(masks_ready, 1)
            dve.tensor_scalar(wx[:, :, :], wx[:, :, :], 0.5, None, ALU.mult)
            dve.tensor_scalar(wout[:, :, :], wout[:, :, :], 0.25, None, ALU.mult)
            dve.tensor_copy(base[:, :], base0)
            dve.wait_ge(a_exp, 1)
            dve.tensor_scalar(a_neg[:, :], a_neg[:, :], -1.0, None, ALU.mult).then_inc(consts_ready, 1)

            dve.wait_ge(consts_ready, 1)
            ln_stats_of(Pair(0, 0))
            ln_apply(Pair(0, 0), first=True)
            step(Pair(0, -1), True, False, "first")
            step(Pair(0, 0), True, True, True)
            with dve.Fori(0, NPAIR // 2 - 2) as i:
                step(Pair(i, 1), True, True, True)
                step(Pair(i, 2), True, True, True)
            step(Pair(0, NPAIR - 3), True, True, True)
            step(Pair(0, NPAIR - 2), True, True, False)
            step(Pair(0, NPAIR - 1), False, True, False)

            ch = Chain(dve, table_step, Pair(0, 0), 0)
            ch.k = 3
            zero_f, cnt, ntf, end = tmp[0][:, 0:E], tmp[0][:, E:2 * E], tmp[0][:, 2 * E:3 * E], tmp[0][:, 3 * E:4 * E]
            ch.did(dve.memset(zero[:, 0:DM], 0.0))
            ch.did(dve.memset(zero[:, DM:XS_W], float(NO_TOKEN)))
            ch.did(dve.memset(zero_f, 1.0))
            ch.did(dve.tensor_tensor(cnt, base[:, :], base0, ALU.subtract))
            ch.last()
            dve.tensor_tensor(pad_i[:, :], base[:, :], pad_row, ALU.add).then_inc(pads_ready, 1)
            ch.did(dve.tensor_scalar(cnt_i[:, :], cnt, float(P - 1), None, ALU.add))
            ch.last()
            ch.did(dve.tensor_scalar(cnt_i[:, :], cnt_i[:, :], 7, None, ALU.arith_shift_right))
            ch.last()
            ch.did(dve.tensor_copy(ntf, cnt_i[:, :]))
            ch.last()
            ch.did(dve.tensor_tensor_scan(end, zero_f, ntf, 0.0, ALU.mult, ALU.add))
            ch.last()
            e_j, first, t3 = tmp[1], tmp[2], tmp[3]
            ch.did(dve.memset(e_j, 0.0))
            ch.did(dve.memset(first, 0.0))
            for e in range(E):
                ch.last()
                ch.did(dve.scalar_tensor_tensor(e_j, tile_no, end[:, e:e + 1], e_j, ALU.is_ge, ALU.add))
                ch.did(dve.tensor_scalar(t3, tile_no, end[:, e:e + 1], ntf[:, e:e + 1], ALU.is_ge, ALU.mult))
                ch.last()
                ch.did(dve.tensor_tensor(first, first, t3, ALU.add))
            ch.last()
            ch.did(dve.tensor_tensor(t3, tile_no, first, ALU.subtract))
            ch.did(dve.tensor_scalar(tmp[4], e_j, float(CAP), None, ALU.mult))
            ch.did(dve.tensor_scalar(tmp[5], e_j, float(E - 1), float(KD * DM), ALU.min, ALU.mult))
            ch.did(dve.tensor_scalar(tmp[6], e_j, float(E - 1), float(DM), ALU.min, ALU.mult))
            ch.last()
            ch.did(dve.scalar_tensor_tensor(t3, t3, float(P), tmp[4], ALU.mult, ALU.add))
            ch.last()
            ch.did(dve.tensor_scalar(tile_i[0:1, 0:NT], t3[0:1, :], float(DUMMY), None, ALU.min))
            ch.did(dve.tensor_copy(tile_i[0:1, NT:2 * NT], tmp[5][0:1, :]))
            ch.did(dve.tensor_copy(tile_i[0:1, 2 * NT:3 * NT], tmp[6][0:1, :]))
            ch.last()
            dve.memset(signal[:, 0:1], 0.0).then_inc(table_ready, 1)
            dve.memset(signal[:, 1:2], 0.0).then_inc(main_done, 1)

            for b in range(4):
                dve.memset(signal[:, 2 + b:3 + b], 0.0).then_inc(t_sum, 1)
            dve.wait_ge(table_ready, 1)
            with dve.Fori(0, NT // TILE_RING) as i:
                for r in range(TILE_RING):
                    col = dve.value_load(tile_i[0:1, bass.ds(i * TILE_RING + (2 * NT + r), 1)], min_val=0, max_val=(E - 1) * DM)
                    dve.wait_ge(xs_got[r], i * 16 + 16)
                    dve.tensor_copy(tok_i[r], xs_t[r][:, DM:XS_W]).then_inc(t_tok, 1)
                    dve.wait_ge(rs_got[r], i * 16 + 16)
                    dve.wait_ge(ew_loaded, 32)
                    dve.tensor_tensor(rs_t[r], rs_t[r], eb_sb[:, bass.ds(col, DM)], ALU.add).then_inc(t_biased, 1)
                    dve.wait_ge(t_biased, i * TILE_RING + (r + 1))
                    dve.wait_ge(t_product, i * TILE_RING + (r + 1))
                    dve.tensor_tensor(rs_t[r], prod[r % 4][:, 0:DM], rs_t[r], ALU.add).then_inc(t_sum, 1)

        @block.gpsimd
        def _(pool):
            def rstd_of(l):
                after(pool, ln_mv, l.count(1, 1))
                pass_waits(pool, pool_passed)
                pool.tensor_scalar(var_eps[:, :], mv[:, :, 1], EPS, None, ALU.add).then_inc(var_ready, 1)
                after(pool, var_ready, l.count(1, 1))
                pool.tensor_tensor(rstd[:, :], var_eps[:, :], neg_half[:, :], ALU.pow).then_inc(rstd_ready, 1)

            def state_products(m):
                after(pool, softplus_step, m.count(SOFTPLUS, SOFTPLUS))
                pool.tensor_tensor(bdt[:, :, :], bc[:, 0, :, :], sp[4][:, :].unsqueeze(2).to_broadcast([P, QB, DS]),
                                   ALU.mult).then_inc(bdt_ready, 1)
                after(pool, split_ready, m.count(2, 2))
                after(pool, bdt_ready, m.count(1, 1))
                pool.tensor_tensor(dta[:, :, :], bdt[:, :, :], bc[:, 1, :, :], ALU.mult).then_inc(bdtc_ready, 1)

            def silu_x(m, v):
                after(pool, thx_ready, m.count(2 * CD, v + 1))
                part = xc[m.par][:, v % CD, v // CD, :]
                pool.tensor_tensor(part, part, th_x[v % 2][:, :], ALU.mult).then_inc(xc_ready, 1)

            def scatter(dst, rows_sb, pair, sent, blocks=range(QB)):
                for q in blocks:
                    pool.indirect_dma_start(dst, bass.IndirectOffsetOnAxis(ap=pos[pair.par][:, q:q + 1], axis=0),
                                            rows_sb[:, q, :], None).then_inc(sent, 16)

            def step(n, do_ab, do_cd, do_ln, before=True):
                m, l = n.plus(1), n.plus(2)
                if before:
                    after(pool, yout_done, n.plus(-1).count(YOUT, YOUT))
                    pass_waits(pool, pool_passed)
                for v in range(2 * CD):
                    if do_ab:
                        silu_x(m, v)
                    if before:
                        scatter(rs_dram[:, :], res, n.plus(-1), rs_sent[1 - n.par], [v])
                if do_ln:
                    rstd_of(l)
                if do_ab:
                    state_products(m)
                    after(pool, pos_ready, m.count(1, 1))
                    pass_waits(pool, pool_passed)
                    scatter(xs_dram[:, :], xn[m.par], m, xs_sent[m.par])

            pool.memset(neg_half[:, :], -0.5).then_inc(pool_consts, 1)
            pool.memset(ones[:, :], 1.0).then_inc(pool_consts, 1)
            pool.wait_ge(pool_consts, 2)
            rstd_of(Pair(0, 0))
            step(Pair(0, -1), True, False, True, False)
            step(Pair(0, 0), True, True, True, False)
            with pool.Fori(0, NPAIR // 2 - 2) as i:
                step(Pair(i, 1), True, True, True)
                step(Pair(i, 2), True, True, True)
            step(Pair(0, NPAIR - 3), True, True, True)
            step(Pair(0, NPAIR - 2), True, True, False)
            step(Pair(0, NPAIR - 1), False, True, False)
            after(pool, yout_done, Pair(0, NPAIR - 1).count(YOUT, YOUT))
            scatter(rs_dram[:, :], res, Pair(0, NPAIR - 1), rs_sent[1])

            pool.wait_ge(pads_ready, 1)
            for dst, w in ((xs_dram, XS_W), (rs_dram, DM)):
                for e in range(E):
                    pool.indirect_dma_start(dst[:, :], bass.IndirectOffsetOnAxis(ap=pad_i[:, e:e + 1], axis=0),
                                            zero[:, 0:w], None).then_inc(pads_sent, 16)
                pool.dma_start(dst[DUMMY:NR, :], zero[:, 0:w]).then_inc(pads_sent, 16)

            with pool.Fori(0, NT // TILE_RING) as i:
                for r in range(TILE_RING):
                    pool.wait_ge(t_tok, i * TILE_RING + (r + 1))
                    pool.wait_ge(t_sum, i * TILE_RING + (r + 5))
                    pass_waits(pool, pool_passed)
                    pool.indirect_dma_start(out[:, :], bass.IndirectOffsetOnAxis(ap=tok_i[r], axis=0), rs_t[r], None,
                                            bounds_check=T - 1, oob_is_err=False).then_inc(out_sent[r], 16)
            for r in range(TILE_RING):
                pool.wait_ge(out_sent[r], 16 * (NT // TILE_RING))


def kernel(L0_attn_x, L0_attn_W_in, L0_attn_conv_w, L0_attn_conv_b, L0_attn_W_x, L0_attn_A_log, L0_attn_D, L0_attn_W_out,
           L0_ffn_gate_w, L0_ffn_gate_b, L0_ffn_expert_w, L0_ffn_expert_b):
    import concourse.bacc as bacc
    from concourse.bass_utils import run_bass_kernel_spmd

    x = np.ascontiguousarray(L0_attn_x).reshape(-1, DM)
    T = x.shape[0]
    smap, mask, ident, upper, code, reset = shape_constants()
    p = np.arange(P, dtype=np.float32)[:, None]
    q = np.arange(QB, dtype=np.float32)[None, :]
    e = np.arange(E, dtype=np.float32)[None, :]
    full = lambda v: np.broadcast_to(v, (P, v.shape[-1]))
    rows = np.concatenate([full(code[None]), full(reset[None]), full(e * (T + P) - 1), q * P + p, q * P + p + QB * P,
                           full(np.arange(T // P + E, dtype=np.float32)[None]), full(0 * e) + p + 1], 1).astype(np.float32)
    conv = np.concatenate([np.asarray(L0_attn_conv_w)[:, 0, :], np.asarray(L0_attn_conv_b)[:, None],
                           np.asarray(L0_attn_D)[:, None]], 1)
    arrays = {
        "x": x,
        "w_in": np.asarray(L0_attn_W_in).T,
        "w_x": np.asarray(L0_attn_W_x).T,
        "w_out": np.asarray(L0_attn_W_out).T,
        "conv": conv,
        "a_row": np.broadcast_to(np.asarray(L0_attn_A_log)[None], (P, DS)),
        "gate_w": np.asarray(L0_ffn_gate_w),
        "gate_b": np.asarray(L0_ffn_gate_b)[:, None],
        "ew": np.asarray(L0_ffn_expert_w),
        "eb": np.broadcast_to(np.asarray(L0_ffn_expert_b).reshape(1, -1), (P, E * DM)),
        "smap": smap, "mask": mask, "ident_d": ident, "upper_d": upper, "rows_d": rows,
    }
    nc = bacc.Bacc("TRN2", target_bir_lowering=False, num_devices=1)
    args, feed = {}, {}
    for name, a in arrays.items():
        a = np.ascontiguousarray(a)
        feed[f"in_{name}"] = a
        args[name] = nc.dram_tensor(f"in_{name}", a.shape, mybir.dt.from_np(a.dtype), kind="ExternalInput").ap()
    out = nc.dram_tensor("out_x", [T, DM], F32, kind="ExternalOutput").ap()
    mamba_moe(nc, out=out, **args)
    r = run_bass_kernel_spmd(nc, [feed], core_ids=[0])
    return r.results[0]["out_x"].reshape(L0_attn_x.shape)
```

```python
from contextlib import ExitStack

import numpy as np

import concourse.bass as bass
from concourse import mybir

P = 128
F32 = mybir.dt.float32
F32R = mybir.dt.float32r
BF16 = mybir.dt.bfloat16
I32 = mybir.dt.int32
U8 = mybir.dt.uint8
ALU = mybir.AluOpType
ACT = mybir.ActivationFunctionType
AX = mybir.AxisListType
EPS = 1e-5

L = 512
DM = 256
DI = 512
DS = 64
DC = 4
E = 8
KB = L // P
QB = 2 * KB
KD = DM // P
CD = DI // P
LEVELS = 7
MAPS = LEVELS + 2
XS_W = DM + 1
NO_TOKEN = 1 << 20

PROJ = 2 * KD + 4 * CD
STAGE_B, STAGE_C = 21, 12
STAGE = STAGE_B + STAGE_C
B_LOGIT, B_BC, B_CT, B_LGT, B_BT, B_EXP, B_RANK = 0, 2, 5, 6, 7, 8, 20
C_TRA, C_XA, C_XB, C_TRB = 21, 25, 27, 29
LEV = 2 * LEVELS
YOUT = 2 * CD + 4
SOFTPLUS = 14
ROUTE = 10
KX = 4
TILE_RING = 8
UNITS = [(0, 0, 0), (0, 0, 1), (0, 1, 1), (0, 1, 0), (0, 2, 0), (0, 2, 1), (0, 3, 1), (0, 3, 0),
         (1, 0, 0), (1, 0, 1), (1, 1, 1), (1, 1, 0), (1, 2, 0), (1, 2, 1), (1, 3, 0), (1, 3, 1)]
LAG = 2
X_UNIT = [UNITS.index((v // CD, v % CD, 0)) for v in range(2 * CD)]


def shape_constants():
    t = np.arange(P)
    smap = np.zeros((P, MAPS, P), np.float32)
    mask = np.zeros((P, LEVELS, P // 2), np.float32)
    src, dst = t[:, None], t[None, :]
    for l in range(LEVELS):
        h = 1 << l
        mid = dst // (2 * h) * (2 * h) + h
        left = dst < mid
        smap[:, l] = np.where(left, (src > dst) & (src < mid), (src >= mid) & (src <= dst))
        right = t[t % (2 * h) >= h][None, :]
        mask[:, l] = (src // (2 * h) == right // (2 * h)) & (src % (2 * h) < h)
    smap[:, LEVELS] = src > dst
    smap[:, LEVELS + 1] = src <= dst
    ident = np.eye(P, dtype=np.float32)
    upper = (src < dst).astype(np.float32)
    code = np.tile(E - np.arange(E, dtype=np.float32), QB)
    reset = np.tile((np.arange(QB) > 0).astype(np.float32), E)
    return smap.reshape(P, -1), mask.reshape(P, -1), ident, upper, code, reset


class Pair:

    def __init__(self, i, off):
        self.i, self.off, self.par = i, off, off % 2

    def plus(self, d):
        return Pair(self.i, self.off + d)

    def count(self, per, k):
        return self.i * (2 * per) + (self.off * per + k)

    def visits(self, per, k=0):
        return self.i * per + (self.off // 2 * per + k)


def after(eng, sem, value):
    if not isinstance(value, int) or value > 0:
        eng.wait_ge(sem, value)


def pass_waits(eng, sem):
    eng.sem_inc(sem, 1)


class Chain:

    def __init__(self, eng, sem, pair, per):
        self.eng, self.sem, self.pair, self.per, self.k = eng, sem, pair, per, 0

    def did(self, ins):
        ins.then_inc(self.sem, 1)
        self.k += 1

    def last(self):
        after(self.eng, self.sem, self.pair.count(self.per, self.k))


def mamba_moe(nc, x, w_in, w_x, w_out, conv, a_row, gate_w, gate_b, ew, eb, smap, mask, ident_d, upper_d,
              rows_d, out):
    T = x.shape[0]
    NPAIR = T // (P * QB)
    CAP = T + P
    DUMMY = E * CAP
    NR = DUMMY + P
    NT = T // P + E
    assert NPAIR % 2 == 0 and NPAIR >= 6 and NT % TILE_RING == 0

    xs_dram = nc.dram_tensor("xs_dram", [NR, XS_W], F32, kind="Internal").ap()
    rs_dram = nc.dram_tensor("rs_dram", [NR, DM], F32, kind="Internal").ap()
    x_pair = x.rearrange("(n q p) d -> n p q d", p=P, q=QB)

    with ExitStack() as ctx:
        def sb(name, shape, dt=F32):
            return ctx.enter_context(nc.sbuf_tensor(name, shape, dt))

        def sb_two(name, shape, other, other_shape):
            at = nc.sbuf_base
            return sb(name, shape), nc.alloc_sbuf_tensor_at(other, other_shape, F32R, offset=at)

        def sem(name):
            return ctx.enter_context(nc.semaphore(name))

        def banks(name):
            return [ctx.enter_context(nc.psum_tensor(f"{name}{i}", [P, 512], F32)) for i in range(2)]

        xn = [sb(f"xn{i}", [P, QB, XS_W]) for i in range(2)]
        stats = sb("stats", [P, QB, 6])
        mv = sb("mv", [P, QB, 2])
        var_eps = sb("var_eps", [P, QB])
        rstd = sb("rstd", [P, QB])
        neg_half = sb("neg_half", [P, QB])
        xt_hi = sb("xt_hi", [P, KD, 2, L], F32R)
        xt_lo = sb("xt_lo", [P, KD, 2, L], F32R)
        part = [P, CD, 2, L]
        xc, gy_hi = zip(*(sb_two(f"xc{i}", part, f"gy_hi{i}", part) for i in range(2)))
        gz, gy_lo = zip(*(sb_two(f"gz{i}", part, f"gy_lo{i}", part) for i in range(2)))
        bc = sb("bc", [P, 2, QB, DS])
        raw_dt = sb("raw_dt", [P, QB])
        sp = [sb(f"sp{i}", [P, QB]) for i in range(8)]
        dta = sb("dta", [P, QB, DS])
        th_x, (dta_hi, dta_lo) = zip(*(sb_two(f"th_x{i}", [P, L], f"dta_{i}", [P, QB, DS]) for i in range(2)))
        bdt = sb("bdt", [P, QB, DS])
        diag = sb("diag", [P, QB])
        bt = sb("bt", [P, L])
        ct = sb("ct", [P, L])
        fac = sb("fac", [P, MAPS, L])
        tot = sb("tot", [P, 2])
        kx = sb("kx", [P, 2 * P])
        xct = sb("xct", [P, KB, DI])
        gm = sb("gm", [P, 2, KB * L])
        res = sb("res", [P, QB, DM])
        lgt = sb("lgt", [E, 2, L])
        lg = sb("lg", [P, QB, E])
        eq = sb("eq", [P, QB, E])
        oh = sb("oh", [P, E, QB])
        cs = sb("cs", [P, E, QB])
        mx = sb("mx", [P, QB])
        sel = sb("sel", [P, QB])
        rt = sb("rt", [P, E], BF16)
        rk = sb("rk", [P, 2 * E])
        base = sb("base", [P, E])
        b1 = sb("b1", [P, E])
        posf = sb("posf", [P, QB])
        pos = [sb(f"pos{i}", [P, QB], I32) for i in range(2)]
        win_hi = sb("win_hi", [P, KD, 2 * DI], F32R)
        win_lo = sb("win_lo", [P, KD, 2 * DI], F32R)
        wx = sb("wx", [P, CD, 2 * DS + 1])
        wout_hi = sb("wout_hi", [P, CD, DM], F32R)
        wout_lo = sb("wout_lo", [P, CD, DM], F32R)
        gate_hi = sb("gate_hi", [P, KD, P], F32R)
        gate_lo = sb("gate_lo", [P, KD, P], F32R)
        smap_r = sb("smap_r", [P, MAPS * P], F32R)
        masks = sb("masks", [P, LEVELS * P // 2], U8)
        ident = sb("ident", [P, P])
        rows = sb("rows", [P, rows_d.shape[1]])
        upper = sb("upper", [P, P], BF16)
        ones = sb("ones", [P, P], BF16)
        convs = sb("convs", [P, CD, DC + 2])
        a_neg = sb("a_neg", [P, DS])
        gb = sb("gb", [E, 1])

        proj_bank, stage_bank, level_bank, yout_bank = (banks(n) for n in ("proj", "stage", "level", "yout"))

        code = rows[:, 0:QB * E].rearrange("p (k e) -> p k e", e=E)
        reset = rows[:, 64:128]
        base0 = rows[:, 128:136]
        tok0 = [rows[:, 136:144], rows[:, 144:152]]
        tile_no = rows[:, 152:152 + NT]
        pad_row = rows[:, 152 + NT:160 + NT]
        gm_flat, fac_flat = (v[:, :, :].rearrange("p a n -> p (a n)") for v in (gm, fac))
        w_stage = gm_flat[:, 0:KD * 2 * DI].rearrange("p (k n) -> p k n", k=KD)
        g_stage = gm_flat[:, KD * 2 * DI:KD * (2 * DI + E)].rearrange("p (k n) -> p k n", k=KD)
        wo_stage = gm_flat[:, KD * (2 * DI + E):KD * (2 * DI + E) + CD * DM].rearrange("p (c n) -> p c n", c=CD)
        up_stage, smap_stage = fac_flat[:, 0:P], fac_flat[:, P:P + MAPS * P]
        mask_stage = fac_flat[:, 2 * P + MAPS * P:2 * P + MAPS * P + LEVELS * P // 2]

        small_loaded, win_loaded, large_loaded, win_split, large_ready, pool_consts = map(
            sem, ("small_loaded", "win_loaded", "large_loaded", "win_split", "large_ready", "pool_consts"))
        x_loaded = [sem(f"x_loaded{i}") for i in range(2)]
        xs_sent = [sem(f"xs_sent{i}") for i in range(2)]
        rs_sent = [sem(f"rs_sent{i}") for i in range(2)]
        res_loaded = sem("res_loaded")
        ln_stats, ln_mv, var_ready, rstd_ready, xn_ready = map(
            sem, ("ln_stats", "ln_mv", "var_ready", "rstd_ready", "xn_ready"))
        proj_full, proj_done, hi_ready = map(sem, ("proj_full", "proj_done", "hi_ready"))
        tap_ready, conv_step, thx_ready, thz_ready, xc_ready = map(
            sem, ("tap_ready", "conv_step", "thx_ready", "thz_ready", "xc_ready"))
        stage_full, stage_copied = map(sem, ("stage_full", "stage_copied"))
        level_full, level_done, gm_cleared = map(sem, ("level_full", "level_done", "gm_cleared"))
        yout_full, yout_done, gated = map(sem, ("yout_full", "yout_done", "gated"))
        softplus_step, exp_ready, dta_ready, split_ready = map(
            sem, ("softplus_step", "exp_ready", "dta_ready", "split_ready"))
        bdt_ready, bdtc_ready, diag_ready, kq_ready, kx_step = map(
            sem, ("bdt_ready", "bdtc_ready", "diag_ready", "kq_ready", "kx_step"))
        route_step, counted, pos_ready = map(sem, ("route_step", "counted", "pos_ready"))

        free_early = gz[0][:, :, :, :].rearrange("p a b n -> p (a b n)")
        free_late = xc[1][:, :, :, :].rearrange("p a b n -> p (a b n)")
        ew_sb = xc[0][:, :, :, :].rearrange("p a b n -> p (a b n)")
        eb_sb = free_early[:, 0:E * DM]
        tmp = [free_early[:, E * DM + r * NT:E * DM + (r + 1) * NT] for r in range(7)]
        zero = free_early[:, E * DM + 7 * NT:E * DM + 7 * NT + XS_W]
        xs_t = [xn[0][:, r, :] for r in range(TILE_RING)]
        rs_t = [free_late[:, r * DM:(r + 1) * DM] for r in range(TILE_RING)]
        xt_t = [free_late[:, (TILE_RING + r) * DM:(TILE_RING + r + 1) * DM] for r in range(2)]
        prod = yout_bank + level_bank
        tok_i = [pos[0][:, r:r + 1] for r in range(TILE_RING)]
        signal = sb("signal", [1, 8])
        pad_i = sb("pad_i", [P, E], I32)
        tile_i = sb("tile_i", [1, 3 * NT], I32)
        cnt_i = sb("cnt_i", [P, E], I32)
        table_step, table_ready, pads_ready, pads_sent = map(
            sem, ("table_step", "table_ready", "pads_ready", "pads_sent"))
        ew_loaded = sem("ew_loaded")
        tanh_ready, wout_split, y_gated, y_high = map(sem, ("tanh_ready", "wout_split", "y_gated", "y_high"))
        dve_passed, pool_passed = map(sem, ("dve_passed", "pool_passed"))
        a_exp = sem("a_exp")
        xs_got = [sem(f"xs_got{r}") for r in range(TILE_RING)]
        rs_got = [sem(f"rs_got{r}") for r in range(TILE_RING)]
        out_sent = [sem(f"out_sent{r}") for r in range(TILE_RING)]
        t_turned, t_copied, t_product, t_biased, t_tok, t_sum = map(
            sem, ("t_turned", "t_copied", "t_product", "t_biased", "t_tok", "t_sum"))

        def of_tiles(engine, first, most):
            return nc.values_load_multi_w_load_instructions(tile_i[0:1, bass.ds(first, TILE_RING)], engines=[engine],
                                                            min_val=0, max_val=most)[1]

        block = ctx.enter_context(nc.Block())

        def blk(ap, ab, j):
            return ap[:, :, ab, j * P:(j + 1) * P]

        @block.sync
        def _(sp_eng):
            sp_eng.dma_start(xn[0][:, :, 0:DM], x_pair[0]).then_inc(x_loaded[0], 16)
            small = [(ident[:, :], ident_d), (rows[:, :], rows_d), (a_neg[:, :], a_row), (gb[:, :], gate_b),
                     (convs[:, :, :], conv.rearrange("(c p) n -> p c n", p=P)),
                     (g_stage, gate_w.rearrange("(k p) n -> p k n", p=P))]
            for dst, src in small:
                sp_eng.dma_start(dst, src).then_inc(small_loaded, 16)
            sp_eng.dma_start(w_stage, w_in.rearrange("(k p) n -> p k n", p=P)).then_inc(win_loaded, 16)
            large = [(wx[:, :, :], w_x.rearrange("(c p) n -> p c n", p=P)),
                     (wo_stage, w_out.rearrange("(c p) n -> p c n", p=P)),
                     (up_stage, upper_d), (smap_stage, smap), (mask_stage, mask)]
            for dst, src in large:
                sp_eng.dma_start(dst, src).then_inc(large_loaded, 16)
            sp_eng.dma_start(xn[1][:, :, 0:DM], x_pair[1]).then_inc(x_loaded[1], 16)
            sp_eng.dma_start(res[:, :, :], x_pair[0]).then_inc(res_loaded, 16)

            def pair_loads(n):
                nxt = n.plus(2)
                after(sp_eng, xs_sent[n.par], n.visits(16 * QB, 16 * QB))
                sp_eng.dma_start(xn[n.par][:, :, 0:DM], x_pair[nxt.i * 2 + nxt.off]).then_inc(x_loaded[n.par], 16)
                after(sp_eng, rs_sent[n.par], n.visits(16 * QB, 16 * QB))
                sp_eng.dma_start(res[:, :, :], x_pair[n.i * 2 + n.off + 1]).then_inc(res_loaded, 16)

            with sp_eng.Fori(0, NPAIR // 2 - 1) as i:
                pair_loads(Pair(i, 0))
                pair_loads(Pair(i, 1))
            after(sp_eng, rs_sent[0], 16 * QB * (NPAIR // 2))
            sp_eng.dma_start(res[:, :, :], x_pair[NPAIR - 1]).then_inc(res_loaded, 16)

            sp_eng.wait_ge(yout_done, YOUT * (NPAIR - 1))
            sp_eng.dma_start(ew_sb.rearrange("p (e k n) -> p e k n", e=E, k=KD),
                             ew.rearrange("e (k p) n -> p e k n", p=P)).then_inc(ew_loaded, 16)
            sp_eng.dma_start(eb_sb, eb).then_inc(ew_loaded, 16)
            for par in range(2):
                sp_eng.wait_ge(xs_sent[par], 16 * QB * (NPAIR // 2))
            sp_eng.wait_ge(pads_sent, 32 * (E + 1))
            sp_eng.wait_ge(table_ready, 1)

            def load_xs(row, r):
                sp_eng.dma_start(xs_t[r], xs_dram[bass.ds(row, P), :]).then_inc(xs_got[r], 16)

            def load_rs(row, r):
                sp_eng.dma_start(rs_t[r], rs_dram[bass.ds(row, P), :]).then_inc(rs_got[r], 16)

            row = of_tiles(mybir.EngineType.SP, 0, NR - P)
            for r in range(TILE_RING):
                load_xs(row[r], r)
            for par in range(2):
                sp_eng.wait_ge(rs_sent[par], 16 * QB * (NPAIR // 2))
            for r in range(TILE_RING):
                load_rs(row[r], r)
            with sp_eng.Fori(0, NT // TILE_RING - 1) as i:
                row = of_tiles(mybir.EngineType.SP, i * TILE_RING + TILE_RING, NR - P)
                for r in range(TILE_RING):
                    sp_eng.wait_ge(out_sent[r], i * 16 + 16)
                    load_xs(row[r], r)
                    load_rs(row[r], r)

        @block.tensor
        def _(pe):
            class Use:
                def __init__(self, banks, full, done):
                    self.banks, self.full, self.done = banks, full, done

                def begin(self, pair, per, k):
                    after(pe, self.done, pair.count(per, k - 1))
                    return self.banks[(pair.off * per + k) % 2]

            proj = Use(proj_bank, proj_full, proj_done)
            stage = Use(stage_bank, stage_full, stage_copied)
            level = Use(level_bank, level_full, level_done)
            yout = Use(yout_bank, yout_full, yout_done)

            def turn_x(m, ab, k):
                u = ab * KD + k
                if u == 0:
                    after(pe, xn_ready, m.count(1, 1))
                ps = proj.begin(m, PROJ, u)
                for j in range(KB):
                    ins = pe.transpose(ps[:, j * P:(j + 1) * P], xn[m.par][:, ab * KB + j, k * P:(k + 1) * P], ident[:, :])
                ins.then_inc(proj_full, 1)

            def project(m, u):
                ab, c, isz = UNITS[u]
                if u % 8 == 0:
                    pe.wait_ge(win_split, 2)
                    after(pe, proj_done, m.count(PROJ, (ab + 1) * KD))
                ps = proj.begin(m, PROJ, 2 * KD + u)
                w = slice((isz * CD + c) * P, (isz * CD + c + 1) * P)
                n = 0
                for k in range(KD):
                    for wi, xi in ((win_hi, xt_hi), (win_hi, xt_lo), (win_lo, xt_hi)):
                        ins = pe.matmul(ps[:, :], wi[:, k, w], xi[:, k, ab, :], start=(n == 0), stop=(n == 3 * KD - 1))
                        n += 1
                ins.then_inc(proj_full, 1)

            def token_products(m, g):
                if g == 0:
                    pe.wait_ge(large_ready, 1)
                    after(pe, xc_ready, m.count(2 * CD, 2 * CD))
                ps = stage.begin(m, STAGE, B_BC + g)
                w = 2 * DS + 1
                for s, q in enumerate(range(3 * g, min(3 * g + 3, QB))):
                    j, ab = q // 2, q % 2
                    for c in range(CD):
                        ins = pe.matmul(ps[:, s * w:(s + 1) * w], blk(xc[m.par], ab, j)[:, c, :], wx[:, c, :],
                                        start=(c == 0), stop=(c == CD - 1))
                ins.then_inc(stage_full, 1)

            def logits(m, ab):
                ps = stage.begin(m, STAGE, B_LOGIT + ab)
                n = 0
                for k in range(KD):
                    for wi, xi in ((gate_hi, xt_hi), (gate_hi, xt_lo), (gate_lo, xt_hi)):
                        ins = pe.matmul(ps[:, :], wi[:, k, :], xi[:, k, ab, :], start=(n == 0), stop=(n == 3 * KD - 1))
                        n += 1
                ins.then_inc(stage_full, 1)

            def turn_states(m, u, src):
                ps = stage.begin(m, STAGE, u)
                for j in range(KB):
                    ins = pe.transpose(ps[:, j * P:(j + 1) * P], src[:, 2 * j:2 * j + 2, :], ident[:, :])
                ins.then_inc(stage_full, 1)

            def turn_logits(m):
                after(pe, stage_copied, m.count(STAGE, B_LOGIT + 2))
                ps = stage.begin(m, STAGE, B_LGT)
                for q in range(QB):
                    ins = pe.matmul(ps[:, q * E:(q + 1) * E], lgt[:, q // KB, q % KB * P:(q % KB + 1) * P],
                                    ident[0:E, 0:E], start=True, stop=True)
                ins.then_inc(stage_full, 1)

            def exponents(m, e):
                third, j = e // KB, e % KB
                if e == 0:
                    after(pe, split_ready, m.count(2, 2))
                ps = stage.begin(m, STAGE, B_EXP + e)
                w = MAPS // 3 * P
                for n, d in enumerate((dta_hi, dta_lo)):
                    ins = pe.matmul(ps[:, 0:w], d[:, 2 * j:2 * j + 2, :], smap_r[:, third * w:(third + 1) * w],
                                    start=(n == 0), stop=(n == 1))
                ins.then_inc(stage_full, 1)

            def rank(m):
                after(pe, counted, m.count(1, 1))
                ps = stage.begin(m, STAGE, B_RANK)
                pe.matmul(ps[:, 0:E], upper[:, :], rt[:, :], start=True, stop=True)
                pe.matmul(ps[:, E:2 * E], ones[:, :], rt[:, :], start=True, stop=True).then_inc(stage_full, 1)

            def turn_xc(n, ab, j):
                ps = stage.begin(n, STAGE, (C_TRB if ab else C_TRA) + j)
                for c in range(CD):
                    ins = pe.transpose(ps[:, c * P:(c + 1) * P], blk(xc[n.par], ab, j)[:, c, :], ident[:, :])
                ins.then_inc(stage_full, 1)

            def score(n, ab, l):
                after(pe, kq_ready, n.count(LEVELS, l + 1))
                ps = level.begin(n, LEV, ab * LEVELS + l)
                for j in range(KB):
                    kq = fac[ab * DS:(ab + 1) * DS, l, j * P:(j + 1) * P]
                    right = kq.rearrange("p (g t h) -> p g t h", t=2, h=1 << l)[:, :, 1, :]
                    ins = pe.matmul(ps[:, j * P // 2:(j + 1) * P // 2], kq, right, start=True, stop=True)
                ins.then_inc(level_full, 1)

            def cross(n, ab):
                if ab == 0:
                    after(pe, kx_step, n.count(KX, KX))
                s = slice(ab * DS, (ab + 1) * DS)
                pre, suf = fac[s, LEVELS + 1, :], fac[s, LEVELS, :]
                ps = stage.begin(n, STAGE, (C_XB if ab else C_XA))
                pe.matmul(ps[:, 0:P], suf[:, 0:P], pre[:, P:2 * P], start=True, stop=True)
                pe.matmul(ps[:, P:3 * P], pre[:, 0:P], kx[s, :], start=True, stop=True).then_inc(stage_full, 1)
                ps = stage.begin(n, STAGE, (C_XB if ab else C_XA) + 1)
                pe.matmul(ps[:, 0:2 * P], suf[:, P:2 * P], kx[s, :], start=True, stop=True)
                pe.matmul(ps[:, 2 * P:3 * P], suf[:, 2 * P:3 * P], pre[:, 3 * P:4 * P], start=True,
                          stop=True).then_inc(stage_full, 1)

            def product_y(n, ab, c):
                if c == 0:
                    after(pe, level_done, n.count(LEV, (ab + 1) * LEVELS))
                    after(pe, stage_copied, n.count(STAGE, (C_TRB if ab else C_XB)  + (KB if ab else 0)))
                ps = yout.begin(n, YOUT, ab * CD + c)
                for j in range(KB):
                    ins = pe.matmul(ps[:, j * P:L], xct[:, j, c * P:(c + 1) * P],
                                    gm[:, ab, j * L:(j + 1) * L - j * P], start=(j == 0), stop=(j == KB - 1))
                ins.then_inc(yout_full, 1)

            def product_out(n, o):
                ab, half = o // 2, o % 2
                if half == 0:
                    pe.wait_ge(wout_split, 2)
                    after(pe, gated, n.count(2 * CD, (ab + 1) * CD))
                ps = yout.begin(n, YOUT, 2 * CD + o)
                for s in range(2):
                    hi, lo = (blk(v[n.par], ab, 2 * half + s) for v in (gy_hi, gy_lo))
                    k = 0
                    for c in range(CD):
                        for g, w in ((hi, wout_hi), (lo, wout_hi), (hi, wout_lo)):
                            ins = pe.matmul(ps[:, s * DM:(s + 1) * DM], g[:, c, :], w[:, c, :],
                                            start=(k == 0), stop=(k == 3 * CD - 1))
                            k += 1
                ins.then_inc(yout_full, 1)

            def step(n, do_ab, do_cd):
                m = n.plus(1)
                if do_ab:
                    turn_x(m, 0, 0), turn_x(m, 0, 1)
                if do_cd:
                    for j in range(KB):
                        turn_xc(n, 0, j)
                if do_ab:
                    turn_x(m, 1, 0), turn_x(m, 1, 1)
                for u in range(8):
                    if do_cd and u < LEVELS:
                        score(n, 0, u)
                    if do_ab:
                        project(m, u)
                if do_cd:
                    cross(n, 0), cross(n, 1)
                for u in range(8):
                    if do_ab:
                        project(m, 8 + u)
                    if do_cd and u < LEVELS:
                        score(n, 1, u)
                    if do_cd and u % 2:
                        product_y(n, 0, u // 2)
                if do_cd:
                    for j in range(KB):
                        turn_xc(n, 1, j)
                if do_ab:
                    logits(m, 0), logits(m, 1)
                if do_cd:
                    product_y(n, 1, 0), product_y(n, 1, 1)
                if do_ab:
                    for g in range(3):
                        token_products(m, g)
                if do_cd:
                    product_y(n, 1, 2), product_y(n, 1, 3)
                if do_ab:
                    after(pe, stage_copied, m.count(STAGE, B_BC + 3))
                    turn_states(m, B_CT, bc[:, 1, :, :])
                    turn_logits(m)
                    after(pe, bdt_ready, m.count(1, 1))
                    turn_states(m, B_BT, bdt)
                for e in range(12):
                    if do_ab:
                        exponents(m, e)
                    if do_cd and e % 4 == 3:
                        product_out(n, e // 4)
                if do_ab:
                    rank(m)
                if do_cd:
                    product_out(n, 3)

            pe.wait_ge(small_loaded, 16 * 6)
            step(Pair(0, -1), True, False)
            step(Pair(0, 0), True, True)
            with pe.Fori(0, NPAIR // 2 - 2) as i:
                step(Pair(i, 1), True, True)
                step(Pair(i, 2), True, True)
            step(Pair(0, NPAIR - 3), True, True)
            step(Pair(0, NPAIR - 2), True, True)
            step(Pair(0, NPAIR - 1), False, True)

            pe.wait_ge(ew_loaded, 32)
            pe.wait_ge(table_ready, 1)

            def turn_tile(r):
                ps = proj_bank[r % 2]
                pe.transpose(ps[:, 0:P], xs_t[r][:, 0:P], ident[:, :])
                pe.transpose(ps[:, P:2 * P], xs_t[r][:, P:2 * P], ident[:, :]).then_inc(t_turned, 1)

            with pe.Fori(0, NT // TILE_RING) as i:
                col = of_tiles(mybir.EngineType.PE, i * TILE_RING + NT, (E - 1) * KD * DM)
                pe.wait_ge(xs_got[0], i * 16 + 16)
                turn_tile(0)
                for r in range(TILE_RING):
                    if r < TILE_RING - 1:
                        pe.wait_ge(xs_got[r + 1], i * 16 + 16)
                        turn_tile(r + 1)
                    pe.wait_ge(t_copied, i * TILE_RING + (r + 1))
                    pe.wait_ge(t_sum, i * TILE_RING + (r + 1))
                    py = prod[r % 4]
                    for k in range(KD):
                        ins = pe.matmul(py[:, 0:DM], xt_t[r % 2][:, k * P:(k + 1) * P],
                                        ew_sb[:, bass.ds(col[r] + k * DM, DM)], start=(k == 0), stop=(k == KD - 1))
                    ins.then_inc(t_product, 1)

        @block.scalar
        def _(act):
            def staged(pair, k, out_ap, in_ap, fn=ACT.Copy, **kw):
                after(act, stage_full, pair.count(STAGE, k + 1))
                act.activation(out_ap, in_ap, fn, **kw).then_inc(stage_copied, 1)

            def bank(pair, k):
                return stage_bank[(pair.off * STAGE + k) % 2]

            def high_part(m, u):
                after(act, proj_full, m.count(PROJ, u + 1))
                act.activation(xt_hi[:, u % KD, u // KD, :], proj_bank[u % 2][:, :], ACT.Copy).then_inc(hi_ready, 1)

            def unit(m, u):
                ab, c, isz = UNITS[u]
                if u == 0:
                    after(act, yout_full, m.plus(-2).count(YOUT, YOUT))
                after(act, proj_full, m.count(PROJ, 2 * KD + u + 1))
                if isz:
                    act.activation(gz[m.par][:, c, ab, :], proj_bank[u % 2][:, :], ACT.Tanh,
                                   scale=0.5).then_inc(thz_ready, 1)
                else:
                    act.activation(xc[m.par][:, c, ab, :], proj_bank[u % 2][:, :], ACT.Identity,
                                   scale=convs[:, c, DC - 1:DC], bias=convs[:, c, DC:DC + 1]).then_inc(tap_ready, 1)

            def tanh_x(m, v):
                after(act, proj_done, m.count(PROJ, 2 * KD + X_UNIT[v] + 1))
                after(act, xc_ready, m.count(2 * CD, v - 1))
                t = th_x[v % 2][:, :]
                act.activation(t, xc[m.par][:, v % CD, v // CD, :], ACT.Tanh, scale=0.5).then_inc(tanh_ready, 1)
                after(act, tanh_ready, m.count(2 * CD, v + 1))
                act.activation(t, t, ACT.Copy, bias=1.0).then_inc(thx_ready, 1)

            def units(m, us):
                for u in us:
                    unit(m, u)
                    for v in range(2 * CD):
                        if X_UNIT[v] == u - LAG:
                            tanh_x(m, v)

            def gated_high(n, ab, c):
                after(act, y_gated, n.count(2 * CD, ab * CD + c + 1))
                act.activation(gy_hi[n.par][:, c, ab, :], gz[n.par][:, c, ab, :], ACT.Copy).then_inc(y_high, 1)

            def cross_copy(n, ab):
                k = C_XB if ab else C_XA
                after(act, yout_full, n.plus(-1).count(YOUT, (ab + 1) * CD))
                staged(n, k, gm[:, ab, P:L], bank(n, k)[:, 0:3 * P])
                after(act, stage_full, n.count(STAGE, k + 2))
                act.activation(gm[:, ab, L + P:L + 3 * P], bank(n, k + 1)[:, 0:2 * P], ACT.Copy)
                act.activation(gm[:, ab, 2 * L + P:2 * L + 2 * P], bank(n, k + 1)[:, 2 * P:3 * P],
                               ACT.Copy).then_inc(stage_copied, 1)

            def step(n, do_ab, do_cd):
                m = n.plus(1)
                if do_ab:
                    high_part(m, 0), high_part(m, 1)
                if do_cd:
                    for j in range(KB):
                        staged(n, C_TRA + j, xct[:, j, :], bank(n, C_TRA + j)[:, :])
                if do_ab:
                    high_part(m, 2), high_part(m, 3)
                    units(m, range(8))
                if do_cd:
                    cross_copy(n, 0), cross_copy(n, 1)
                if do_ab:
                    units(m, range(8, 11))
                for c in range(CD):
                    if do_cd and c < CD - 1:
                        gated_high(n, 0, c)
                    if do_ab:
                        units(m, range(11 + 2 * c, min(13 + 2 * c, 16)))
                if do_ab:
                    for v in range(2 * CD):
                        if X_UNIT[v] > 15 - LAG:
                            tanh_x(m, v)
                if do_cd:
                    for j in range(KB):
                        staged(n, C_TRB + j, xct[:, j, :], bank(n, C_TRB + j)[:, :])
                if do_ab:
                    w = 2 * DS + 1
                    after(act, bdtc_ready, m.plus(-1).count(1, 1))
                    for ab in range(2):
                        staged(m, B_LOGIT + ab, lgt[:, ab, :], bank(m, B_LOGIT + ab)[0:E, :], ACT.Identity, bias=gb[:, :])
                if do_cd:
                    gated_high(n, 0, CD - 1)
                if do_ab:
                    for g in range(3):
                        nq = min(3, QB - 3 * g)
                        after(act, stage_full, m.count(STAGE, B_BC + g + 1))
                        ps = bank(m, B_BC + g)[:, 0:nq * w].rearrange("p (q n) -> p q n", n=w)
                        for t in range(2):
                            act.activation(bc[:, t, 3 * g:3 * g + nq, :], ps[:, :, t * DS:(t + 1) * DS], ACT.Copy)
                        act.activation(raw_dt[:, 3 * g:3 * g + nq], ps[:, :, 2 * DS], ACT.Copy).then_inc(stage_copied, 1)
                    after(act, softplus_step, m.count(SOFTPLUS, 1))
                    act.activation(sp[1][:, :], sp[0][:, :], ACT.Exp).then_inc(exp_ready, 1)
                if do_cd:
                    gated_high(n, 1, 0), gated_high(n, 1, 1)
                if do_ab:
                    after(act, kx_step, m.plus(-1).count(KX, KX))
                    staged(m, B_CT, ct[:, :], bank(m, B_CT)[:, :])
                    staged(m, B_LGT, lg[:, :, :], bank(m, B_LGT)[:, 0:QB * E].rearrange("p (q e) -> p q e", e=E))
                    staged(m, B_BT, bt[:, :], bank(m, B_BT)[:, :])
                t = MAPS // 3
                for e in range(12):
                    if do_cd and e in (1, 4):
                        gated_high(n, 1, 2 + e // 4)
                    if do_ab:
                        third, j = e // KB, e % KB
                        staged(m, B_EXP + e, fac[:, third * t:(third + 1) * t, j * P:(j + 1) * P],
                               bank(m, B_EXP + e)[:, 0:t * P].rearrange("p (t n) -> p t n", n=P), ACT.Exp)
                if do_ab:
                    staged(m, B_RANK, rk[:, :], bank(m, B_RANK)[:, 0:2 * E])

            act.wait_ge(small_loaded, 16 * 6)
            act.activation(a_neg[:, :], a_neg[:, :], ACT.Exp).then_inc(a_exp, 1)
            act.wait_ge(win_loaded, 16)
            act.activation(win_hi[:, :, :], w_stage, ACT.Copy).then_inc(win_split, 1)
            step(Pair(0, -1), True, False)
            step(Pair(0, 0), True, True)
            with act.Fori(0, NPAIR // 2 - 2) as i:
                step(Pair(i, 1), True, True)
                step(Pair(i, 2), True, True)
            step(Pair(0, NPAIR - 3), True, True)
            step(Pair(0, NPAIR - 2), True, True)
            step(Pair(0, NPAIR - 1), False, True)

            act.wait_ge(yout_full, YOUT * NPAIR)
            with act.Fori(0, NT // TILE_RING) as i:
                for r in range(TILE_RING):
                    act.wait_ge(t_turned, i * TILE_RING + (r + 1))
                    act.activation(xt_t[r % 2], proj_bank[r % 2][:, 0:DM], ACT.Copy).then_inc(t_copied, 1)

        @block.vector
        def _(dve):
            def ln_stats_of(l):
                after(dve, x_loaded[l.par], l.visits(16, 16))
                for q in range(QB):
                    ins = dve.bn_stats(stats[:, q, :], xn[l.par][:, q, 0:DM])
                ins.then_inc(ln_stats, 1)
                after(dve, ln_stats, l.count(1, 1))
                pass_waits(dve, dve_passed)
                for q in range(QB):
                    ins = dve.bn_aggr(mv[:, q, :], stats[:, q, :])
                ins.then_inc(ln_mv, 1)

            def ln_apply(l, first=False):
                after(dve, rstd_ready, l.count(1, 1))
                if first:
                    dve.tensor_copy(xn[l.par][:, :, DM], tok0[l.par])
                else:
                    dve.tensor_scalar(xn[l.par][:, :, DM], xn[l.par][:, :, DM], float(2 * QB * P), None, ALU.add)
                for q in range(QB):
                    v = xn[l.par][:, q, 0:DM]
                    ins = dve.tensor_scalar(v, v, mv[:, q, 0:1], rstd[:, q:q + 1], ALU.subtract, ALU.mult)
                ins.then_inc(xn_ready, 1)

            def low_part(m, u):
                after(dve, hi_ready, m.count(2 * KD, u + 1))
                dve.tensor_tensor(xt_lo[:, u % KD, u // KD, :], proj_bank[u % 2][:, :],
                                  xt_hi[:, u % KD, u // KD, :].bitcast(F32), ALU.subtract).then_inc(proj_done, 1)

            def conv(m, u):
                ab, c, _ = UNITS[u]
                out_c, k = xc[m.par][:, c, ab, :], 2 * (ab * CD + c)
                after(dve, tap_ready, m.count(2 * CD, ab * CD + c + 1))
                for s in range(1, DC):
                    if s > 1:
                        after(dve, conv_step, m.count(4 * CD, k + s - 1))
                    ins = dve.scalar_tensor_tensor(out_c[:, s:L], proj_bank[u % 2][:, 0:L - s],
                                                   convs[:, c, DC - 1 - s:DC - s], out_c[:, s:L], ALU.mult, ALU.add)
                    ins.then_inc(conv_step if s < DC - 1 else proj_done, 1)

            def project(m, u):
                ab, c, isz = UNITS[u]
                if not isz:
                    conv(m, u)
                else:
                    after(dve, thz_ready, m.count(2 * CD, ab * CD + c + 1))
                    part = gz[m.par][:, c, ab, :]
                    dve.scalar_tensor_tensor(part, part, 1.0, proj_bank[u % 2][:, :], ALU.add, ALU.mult).then_inc(proj_done, 1)

            def clear_gm(n, ab):
                if ab == 0:
                    after(dve, diag_ready, n.count(1, 1))
                after(dve, yout_full, n.plus(-1).count(YOUT, (ab + 1) * CD))
                for j in range(KB):
                    ins = dve.tensor_scalar(gm[:, ab, j * L:j * L + P], ident[:, :], diag[:, 2 * j + ab:2 * j + ab + 1],
                                            None, ALU.mult)
                ins.then_inc(gm_cleared, 1)

            def mask_level(n, ab, l):
                u = ab * LEVELS + l
                after(dve, level_full, n.count(LEV, u + 1))
                if l:
                    after(dve, level_done, n.count(LEV, u))
                else:
                    after(dve, gm_cleared, n.count(2, ab + 1))
                dve.wait_ge(large_ready, 1)
                pass_waits(dve, dve_passed)
                h, g, w = 1 << l, P // 2 >> l, P // 2
                right = gm[:, ab, :].rearrange("p (j g t h) -> p j g t h", j=KB, t=2, h=h)[:, :, 0:g, 1, :]
                dve.copy_predicated(right, masks[:, l * w:(l + 1) * w].rearrange("p (g h) -> p g h", h=h).unsqueeze(1)
                                    .to_broadcast([P, KB, g, h]),
                                    level_bank[u % 2][:, 0:KB * w].rearrange("p (j g h) -> p j g h", j=KB, h=h)
                                    ).then_inc(level_done, 1)

            def gate_y(n, ab, c):
                u = ab * CD + c
                y, g = xc[n.par][:, c, ab, :], gz[n.par][:, c, ab, :]
                after(dve, yout_full, n.count(YOUT, u + 1))
                dve.scalar_tensor_tensor(y, y, convs[:, c, DC + 1:DC + 2], yout_bank[u % 2][:, :], ALU.mult,
                                         ALU.add).then_inc(yout_done, 1)
                after(dve, yout_done, n.count(YOUT, u + 1))
                dve.tensor_tensor(g, g, y, ALU.mult).then_inc(y_gated, 1)

            def gated_low(n, ab, c):
                after(dve, y_high, n.count(2 * CD, ab * CD + c + 1))
                g = gz[n.par][:, c, ab, :]
                dve.tensor_tensor(gy_lo[n.par][:, c, ab, :], g, gy_hi[n.par][:, c, ab, :].bitcast(F32), ALU.subtract).then_inc(gated, 1)

            def add_residual(n, o):
                after(dve, yout_full, n.count(YOUT, 2 * CD + o + 1))
                if o == 0:
                    after(dve, res_loaded, n.count(16, 16))
                r = res[:, 2 * o:2 * o + 2, :]
                dve.tensor_tensor(r, yout_bank[o % 2][:, :].rearrange("p (q d) -> p q d", q=2), r,
                                  ALU.add).then_inc(yout_done, 1)

            raw = raw_dt[:, :]

            def softplus_start(m):
                after(dve, stage_copied, m.count(STAGE, B_BC + 3))
                ch = Chain(dve, softplus_step, m, SOFTPLUS)
                ch.did(dve.scalar_tensor_tensor(sp[0][:, :], raw, -1.0, raw, ALU.mult, ALU.min))
                ch.did(dve.tensor_scalar(sp[2][:, :], raw, 0.0, None, ALU.max))
                return ch

            def softplus_end(m, ch):
                after(dve, exp_ready, m.count(1, 1))
                ch.did(dve.tensor_scalar(sp[3][:, :], sp[1][:, :], 2.0, None, ALU.add))
                ch.last()
                ch.did(dve.reciprocal(sp[4][:, :], sp[3][:, :]))
                ch.last()
                ch.did(dve.tensor_tensor(sp[5][:, :], sp[1][:, :], sp[4][:, :], ALU.mult))
                ch.last()
                ch.did(dve.tensor_tensor(sp[6][:, :], sp[5][:, :], sp[5][:, :], ALU.mult))
                ch.last()
                ch.did(dve.tensor_scalar(sp[7][:, :], sp[6][:, :], 1.0 / 13, None, ALU.mult))
                for k in (11, 9, 7, 5, 3):
                    ch.last()
                    ch.did(dve.scalar_tensor_tensor(sp[7][:, :], sp[7][:, :], 1.0 / k, sp[6][:, :], ALU.add, ALU.mult))
                ch.last()
                ch.did(dve.scalar_tensor_tensor(sp[3][:, :], sp[7][:, :], 1.0, sp[5][:, :], ALU.add, ALU.mult))
                ch.last()
                ch.did(dve.scalar_tensor_tensor(sp[4][:, :], sp[3][:, :], 2.0, sp[2][:, :], ALU.mult, ALU.add))
                assert ch.k == SOFTPLUS
                ch.last()
                dve.tensor_tensor(dta[:, :, :], a_neg[:, :].unsqueeze(1).to_broadcast([P, QB, DS]),
                                  sp[4][:, :].unsqueeze(2).to_broadcast([P, QB, DS]), ALU.mult).then_inc(dta_ready, 1)
                after(dve, dta_ready, m.count(1, 1))
                dve.tensor_copy(dta_hi[:, :, :], dta[:, :, :]).then_inc(split_ready, 1)
                after(dve, split_ready, m.count(2, 1))
                dve.tensor_tensor(dta_lo[:, :, :], dta[:, :, :], dta_hi[:, :, :].bitcast(F32),
                                  ALU.subtract).then_inc(split_ready, 1)

            def route_count(m):
                ch = Chain(dve, route_step, m, ROUTE)
                after(dve, stage_copied, m.count(STAGE, B_LGT + 1))
                wide = [P, QB, E]
                ch.did(dve.tensor_reduce(mx[:, :], lg[:, :, :], AX.X, ALU.max))
                ch.last()
                ch.did(dve.tensor_tensor(eq[:, :, :], lg[:, :, :], mx[:, :].unsqueeze(2).to_broadcast(wide), ALU.is_equal))
                ch.last()
                ch.did(dve.tensor_tensor(eq[:, :, :], eq[:, :, :], code, ALU.mult))
                ch.last()
                ch.did(dve.tensor_reduce(sel[:, :], eq[:, :, :], AX.X, ALU.max))
                ch.last()
                ch.did(dve.tensor_tensor(oh[:, :, :].rearrange("p e q -> p q e"), code,
                                         sel[:, :].unsqueeze(2).to_broadcast(wide), ALU.is_equal))
                ch.last()
                ch.did(dve.tensor_tensor_scan(cs[:, :, :].rearrange("p e q -> p (e q)"), reset,
                                              oh[:, :, :].rearrange("p e q -> p (e q)"), 0.0, ALU.mult, ALU.add))
                ch.last()
                dve.tensor_copy(rt[:, :], cs[:, :, QB - 1]).then_inc(counted, 1)
                return ch

            def route_place(m, ch):
                after(dve, stage_copied, m.count(STAGE, B_RANK + 1))
                after(dve, pos_ready, m.count(1, 0))
                ch.did(dve.tensor_tensor(b1[:, :], base[:, :], rk[:, 0:E], ALU.add))
                ch.last()
                ch.did(dve.tensor_tensor(cs[:, :, :], cs[:, :, :], b1[:, :].unsqueeze(2).to_broadcast([P, E, QB]), ALU.add))
                ch.last()
                ch.did(dve.tensor_tensor(cs[:, :, :], cs[:, :, :], oh[:, :, :], ALU.mult))
                ch.last()
                ch.did(dve.tensor_reduce(posf[:, :], cs[:, :, :].rearrange("p e q -> p q e"), AX.X, ALU.add))
                assert ch.k == ROUTE
                dve.tensor_tensor(base[:, :], base[:, :], rk[:, E:2 * E], ALU.add)
                ch.last()
                after(dve, xs_sent[m.par], m.visits(16 * QB))
                after(dve, rs_sent[m.par], m.visits(16 * QB))
                dve.tensor_copy(pos[m.par][:, :], posf[:, :]).then_inc(pos_ready, 1)

            def scale_level(m, l):
                h = 1 << l
                after(dve, stage_copied, m.count(STAGE, B_EXP + (l // (MAPS // 3) + 1) * KB))
                f, b, c = (v.rearrange("p (g t h) -> p g t h", t=2, h=h) for v in (fac[:, l, :], bt[:, :], ct[:, :]))
                dve.tensor_tensor(f[:, :, 0, :], f[:, :, 0, :], b[:, :, 0, :], ALU.mult)
                dve.tensor_tensor(f[:, :, 1, :], f[:, :, 1, :], c[:, :, 1, :], ALU.mult).then_inc(kq_ready, 1)

            def scale_between(m):
                suf, pre = fac[:, LEVELS, :], fac[:, LEVELS + 1, :]
                dve.tensor_copy(tot[:, :], pre.rearrange("p (j n) -> p j n", n=P)[:, 1:3, P - 1]).then_inc(kx_step, 1)
                dve.tensor_tensor(suf, suf, bt[:, :], ALU.mult).then_inc(kx_step, 1)
                after(dve, kx_step, m.count(KX, 1))
                dve.tensor_tensor(pre, pre, ct[:, :], ALU.mult).then_inc(kx_step, 1)
                after(dve, kx_step, m.count(KX, 3))
                dve.tensor_copy(kx[:, 0:P], pre[:, 2 * P:3 * P])
                dve.tensor_scalar(kx[:, P:2 * P], pre[:, 3 * P:4 * P], tot[:, 1:2], None, ALU.mult)
                dve.tensor_scalar(pre[:, 0:P], suf[:, 0:P], tot[:, 0:1], None, ALU.mult).then_inc(kx_step, 1)

            def sum_diag(m):
                after(dve, bdtc_ready, m.count(1, 1))
                dve.tensor_reduce(diag[:, :], dta[:, :, :], AX.X, ALU.add).then_inc(diag_ready, 1)

            def step(n, do_ab, do_cd, do_ln):
                m, l = n.plus(1), n.plus(2)
                if do_ab:
                    low_part(m, 0), low_part(m, 1)
                if do_cd:
                    clear_gm(n, 0)
                if do_ab:
                    low_part(m, 2), low_part(m, 3)
                for u in range(8):
                    if do_cd and u < LEVELS:
                        mask_level(n, 0, u)
                    if do_ab:
                        project(m, u)
                if do_cd:
                    clear_gm(n, 1)
                for u in range(8):
                    if do_ab:
                        project(m, 8 + u)
                    if do_cd and u < LEVELS:
                        mask_level(n, 1, u)
                    if do_cd and u % 2:
                        gate_y(n, 0, u // 2)
                        if u > 1:
                            gated_low(n, 0, u // 2 - 1)
                if do_ln:
                    ln_stats_of(l)
                if do_cd:
                    gate_y(n, 1, 0), gate_y(n, 1, 1)
                    gated_low(n, 0, 3)
                if do_ab:
                    ch = softplus_start(m)
                    softplus_end(m, ch)
                if do_cd:
                    gate_y(n, 1, 2)
                    gated_low(n, 1, 0), gated_low(n, 1, 1)
                if do_ab:
                    ch = route_count(m)
                if do_cd:
                    gate_y(n, 1, 3)
                    gated_low(n, 1, 2)
                if do_ab:
                    sum_diag(m)
                    for lv in range(3):
                        scale_level(m, lv)
                if do_cd:
                    add_residual(n, 0)
                    gated_low(n, 1, 3)
                if do_ab:
                    for lv in range(3, 6):
                        scale_level(m, lv)
                if do_ln:
                    ln_apply(l, first=do_ln == "first")
                if do_cd:
                    add_residual(n, 1)
                if do_ab:
                    scale_level(m, 6)
                    scale_between(m)
                    route_place(m, ch)
                if do_cd:
                    add_residual(n, 2), add_residual(n, 3)

            ln_stats_of(Pair(0, 0))
            dve.memset(gate_hi[:, :, :].bitcast(F32), 0.0)
            dve.memset(gate_lo[:, :, :].bitcast(F32), 0.0).then_inc(table_step, 1)
            dve.wait_ge(small_loaded, 16 * 6)
            dve.wait_ge(table_step, 1)
            dve.tensor_copy(gate_hi[:, :, 0:E], g_stage)
            dve.tensor_copy(base[:, :], base0).then_inc(table_step, 1)
            dve.wait_ge(table_step, 2)
            dve.tensor_tensor(gate_lo[:, :, 0:E], g_stage, gate_hi[:, :, 0:E].bitcast(F32), ALU.subtract)
            dve.wait_ge(a_exp, 1)
            dve.tensor_scalar(a_neg[:, :], a_neg[:, :], -1.0, None, ALU.mult).then_inc(table_step, 1)
            dve.wait_ge(table_step, 3)
            ln_apply(Pair(0, 0), first=True)
            dve.wait_ge(win_split, 1)
            dve.tensor_tensor(win_lo[:, :, :], w_stage, win_hi[:, :, :].bitcast(F32), ALU.subtract).then_inc(win_split, 1)
            step(Pair(0, -1), True, False, "first")
            dve.wait_ge(large_ready, 1)
            dve.tensor_copy(wout_hi[:, :, :], wo_stage).then_inc(wout_split, 1)
            dve.wait_ge(wout_split, 1)
            dve.tensor_tensor(wout_lo[:, :, :], wo_stage, wout_hi[:, :, :].bitcast(F32), ALU.subtract).then_inc(wout_split, 1)
            step(Pair(0, 0), True, True, True)
            with dve.Fori(0, NPAIR // 2 - 2) as i:
                step(Pair(i, 1), True, True, True)
                step(Pair(i, 2), True, True, True)
            step(Pair(0, NPAIR - 3), True, True, True)
            step(Pair(0, NPAIR - 2), True, True, False)
            ch = Chain(dve, table_step, Pair(0, 0), 0)
            ch.k = 3
            ones_row, cnt, ntf, end = tmp[0][:, 0:E], tmp[0][:, E:2 * E], tmp[0][:, 2 * E:3 * E], tmp[0][:, 3 * E:4 * E]
            dve.wait_ge(pos_ready, NPAIR)
            dve.wait_ge(yout_full, YOUT * (NPAIR - 1))
            ch.did(dve.memset(zero[:, 0:DM], 0.0))
            ch.did(dve.memset(zero[:, DM:XS_W], float(NO_TOKEN)))
            ch.did(dve.memset(ones_row, 1.0))
            ch.did(dve.tensor_tensor(cnt, base[:, :], base0, ALU.subtract))
            ch.last()
            dve.tensor_tensor(pad_i[:, :], base[:, :], pad_row, ALU.add).then_inc(pads_ready, 1)
            ch.did(dve.tensor_scalar(cnt_i[:, :], cnt, float(P - 1), None, ALU.add))
            ch.last()
            ch.did(dve.tensor_scalar(cnt_i[:, :], cnt_i[:, :], 7, None, ALU.arith_shift_right))
            ch.last()
            ch.did(dve.tensor_copy(ntf, cnt_i[:, :]))
            ch.last()
            ch.did(dve.tensor_tensor_scan(end, ones_row, ntf, 0.0, ALU.mult, ALU.add))
            ch.last()
            e_j, first, t3 = tmp[1], tmp[2], tmp[3]
            ch.did(dve.memset(e_j, 0.0))
            ch.did(dve.memset(first, 0.0))
            for e in range(E):
                ch.last()
                ch.did(dve.scalar_tensor_tensor(e_j, tile_no, end[:, e:e + 1], e_j, ALU.is_ge, ALU.add))
                ch.did(dve.tensor_scalar(t3, tile_no, end[:, e:e + 1], ntf[:, e:e + 1], ALU.is_ge, ALU.mult))
                ch.last()
                ch.did(dve.tensor_tensor(first, first, t3, ALU.add))
            ch.last()
            ch.did(dve.tensor_tensor(t3, tile_no, first, ALU.subtract))
            ch.did(dve.tensor_scalar(tmp[4], e_j, float(CAP), None, ALU.mult))
            ch.did(dve.tensor_scalar(tmp[5], e_j, float(E - 1), float(KD * DM), ALU.min, ALU.mult))
            ch.did(dve.tensor_scalar(tmp[6], e_j, float(E - 1), float(DM), ALU.min, ALU.mult))
            ch.last()
            ch.did(dve.scalar_tensor_tensor(t3, t3, float(P), tmp[4], ALU.mult, ALU.add))
            ch.last()
            ch.did(dve.tensor_scalar(tile_i[0:1, 0:NT], t3[0:1, :], float(DUMMY), None, ALU.min))
            ch.did(dve.tensor_copy(tile_i[0:1, NT:2 * NT], tmp[5][0:1, :]))
            ch.did(dve.tensor_copy(tile_i[0:1, 2 * NT:3 * NT], tmp[6][0:1, :]))
            ch.last()
            dve.memset(signal[:, 0:1], 0.0).then_inc(table_ready, 1)

            step(Pair(0, NPAIR - 1), False, True, False)

            for b in range(4):
                dve.memset(signal[:, 2 + b:3 + b], 0.0).then_inc(t_sum, 1)
            dve.wait_ge(table_ready, 1)
            with dve.Fori(0, NT // TILE_RING) as i:
                col = of_tiles(mybir.EngineType.DVE, i * TILE_RING + 2 * NT, (E - 1) * DM)
                for r in range(TILE_RING):
                    dve.wait_ge(xs_got[r], i * 16 + 16)
                    dve.tensor_copy(tok_i[r], xs_t[r][:, DM:XS_W]).then_inc(t_tok, 1)
                    dve.wait_ge(rs_got[r], i * 16 + 16)
                    dve.wait_ge(ew_loaded, 32)
                    dve.tensor_tensor(rs_t[r], rs_t[r], eb_sb[:, bass.ds(col[r], DM)], ALU.add).then_inc(t_biased, 1)
                    dve.wait_ge(t_biased, i * TILE_RING + (r + 1))
                    dve.wait_ge(t_product, i * TILE_RING + (r + 1))
                    dve.tensor_tensor(rs_t[r], prod[r % 4][:, 0:DM], rs_t[r], ALU.add).then_inc(t_sum, 1)

        @block.gpsimd
        def _(pool):
            def rstd_of(l):
                after(pool, ln_mv, l.count(1, 1))
                pass_waits(pool, pool_passed)
                pool.tensor_scalar(var_eps[:, :], mv[:, :, 1], EPS, None, ALU.add).then_inc(var_ready, 1)
                after(pool, var_ready, l.count(1, 1))
                pool.tensor_tensor(rstd[:, :], var_eps[:, :], neg_half[:, :], ALU.pow).then_inc(rstd_ready, 1)

            def state_products(m):
                after(pool, softplus_step, m.count(SOFTPLUS, SOFTPLUS))
                pool.tensor_tensor(bdt[:, :, :], bc[:, 0, :, :], sp[4][:, :].unsqueeze(2).to_broadcast([P, QB, DS]),
                                   ALU.mult).then_inc(bdt_ready, 1)
                after(pool, split_ready, m.count(2, 2))
                after(pool, bdt_ready, m.count(1, 1))
                pool.tensor_tensor(dta[:, :, :], bdt[:, :, :], bc[:, 1, :, :], ALU.mult).then_inc(bdtc_ready, 1)

            def silu_x(m, v):
                after(pool, thx_ready, m.count(2 * CD, v + 1))
                part = xc[m.par][:, v % CD, v // CD, :]
                pool.tensor_tensor(part, part, th_x[v % 2][:, :], ALU.mult).then_inc(xc_ready, 1)

            def scatter(dst, rows_sb, pair, sent, blocks=range(QB)):
                for q in blocks:
                    pool.indirect_dma_start(dst, bass.IndirectOffsetOnAxis(ap=pos[pair.par][:, q:q + 1], axis=0),
                                            rows_sb[:, q, :], None).then_inc(sent, 16)

            def step(n, do_ab, do_cd, do_ln, before=True):
                m, l = n.plus(1), n.plus(2)
                if before:
                    after(pool, yout_done, n.plus(-1).count(YOUT, YOUT))
                    pass_waits(pool, pool_passed)
                for v in range(2 * CD):
                    if do_ab:
                        silu_x(m, v)
                    if before:
                        scatter(rs_dram[:, :], res, n.plus(-1), rs_sent[1 - n.par], [v])
                if do_ln:
                    rstd_of(l)
                if do_ab:
                    state_products(m)
                    after(pool, pos_ready, m.count(1, 1))
                    pass_waits(pool, pool_passed)
                    scatter(xs_dram[:, :], xn[m.par], m, xs_sent[m.par])

            pool.memset(neg_half[:, :], -0.5).then_inc(pool_consts, 1)
            pool.memset(ones[:, :], 1.0).then_inc(pool_consts, 1)
            pool.wait_ge(pool_consts, 2)
            rstd_of(Pair(0, 0))
            pool.wait_ge(large_loaded, 16 * 5)
            pool.tensor_scalar(wx[:, :, :], wx[:, :, :], 0.5, None, ALU.mult)
            pool.tensor_scalar(wo_stage, wo_stage, 0.25, None, ALU.mult)
            pool.tensor_copy(upper[:, :], up_stage)
            pool.tensor_copy(smap_r[:, :], smap_stage)
            pool.tensor_copy(masks[:, :], mask_stage).then_inc(large_ready, 1)
            step(Pair(0, -1), True, False, True, False)
            step(Pair(0, 0), True, True, True, False)
            with pool.Fori(0, NPAIR // 2 - 2) as i:
                step(Pair(i, 1), True, True, True)
                step(Pair(i, 2), True, True, True)
            step(Pair(0, NPAIR - 3), True, True, True)
            step(Pair(0, NPAIR - 2), True, True, False)
            step(Pair(0, NPAIR - 1), False, True, False)
            pool.wait_ge(pads_ready, 1)
            for dst, w in ((xs_dram, XS_W), (rs_dram, DM)):
                for e in range(E):
                    pool.indirect_dma_start(dst[:, :], bass.IndirectOffsetOnAxis(ap=pad_i[:, e:e + 1], axis=0),
                                            zero[:, 0:w], None).then_inc(pads_sent, 16)
                pool.dma_start(dst[DUMMY:NR, :], zero[:, 0:w]).then_inc(pads_sent, 16)
            for o in range(QB // 2):
                pool.wait_ge(yout_done, YOUT * (NPAIR - 1) + 2 * CD + o + 1)
                scatter(rs_dram[:, :], res, Pair(0, NPAIR - 1), rs_sent[1], [2 * o, 2 * o + 1])


            with pool.Fori(0, NT // TILE_RING) as i:
                for r in range(TILE_RING):
                    pool.wait_ge(t_tok, i * TILE_RING + (r + 1))
                    pool.wait_ge(t_sum, i * TILE_RING + (r + 5))
                    pass_waits(pool, pool_passed)
                    pool.indirect_dma_start(out[:, :], bass.IndirectOffsetOnAxis(ap=tok_i[r], axis=0), rs_t[r], None,
                                            bounds_check=T - 1, oob_is_err=False).then_inc(out_sent[r], 16)
            for r in range(TILE_RING):
                pool.wait_ge(out_sent[r], 16 * (NT // TILE_RING))


def kernel(L0_attn_x, L0_attn_W_in, L0_attn_conv_w, L0_attn_conv_b, L0_attn_W_x, L0_attn_A_log, L0_attn_D, L0_attn_W_out,
           L0_ffn_gate_w, L0_ffn_gate_b, L0_ffn_expert_w, L0_ffn_expert_b):
    import concourse.bacc as bacc
    from concourse.bass_utils import run_bass_kernel_spmd

    x = np.ascontiguousarray(L0_attn_x).reshape(-1, DM)
    T = x.shape[0]
    smap, mask, ident, upper, code, reset = shape_constants()
    p = np.arange(P, dtype=np.float32)[:, None]
    q = np.arange(QB, dtype=np.float32)[None, :]
    e = np.arange(E, dtype=np.float32)[None, :]
    full = lambda v: np.broadcast_to(v, (P, v.shape[-1]))
    rows = np.concatenate([full(code[None]), full(reset[None]), full(e * (T + P) - 1), q * P + p, q * P + p + QB * P,
                           full(np.arange(T // P + E, dtype=np.float32)[None]), full(0 * e) + p + 1], 1).astype(np.float32)
    conv = np.concatenate([np.asarray(L0_attn_conv_w)[:, 0, :], np.asarray(L0_attn_conv_b)[:, None],
                           np.asarray(L0_attn_D)[:, None]], 1)
    arrays = {
        "x": x,
        "w_in": np.asarray(L0_attn_W_in).T,
        "w_x": np.asarray(L0_attn_W_x).T,
        "w_out": np.asarray(L0_attn_W_out).T,
        "conv": conv,
        "a_row": np.broadcast_to(np.asarray(L0_attn_A_log)[None], (P, DS)),
        "gate_w": np.asarray(L0_ffn_gate_w),
        "gate_b": np.asarray(L0_ffn_gate_b)[:, None],
        "ew": np.asarray(L0_ffn_expert_w),
        "eb": np.broadcast_to(np.asarray(L0_ffn_expert_b).reshape(1, -1), (P, E * DM)),
        "smap": smap, "mask": mask, "ident_d": ident, "upper_d": upper, "rows_d": rows,
    }
    nc = bacc.Bacc("TRN2", target_bir_lowering=False, num_devices=1)
    args, feed = {}, {}
    for name, a in arrays.items():
        a = np.ascontiguousarray(a)
        feed[f"in_{name}"] = a
        args[name] = nc.dram_tensor(f"in_{name}", a.shape, mybir.dt.from_np(a.dtype), kind="ExternalInput").ap()
    out = nc.dram_tensor("out_x", [T, DM], F32, kind="ExternalOutput").ap()
    mamba_moe(nc, out=out, **args)
    r = run_bass_kernel_spmd(nc, [feed], core_ids=[0])
    return r.results[0]["out_x"].reshape(L0_attn_x.shape)
```
